# Optimizing a Trainium2 kernel written in Bass

```python
import numpy as np
import jax
import jax.numpy as jnp

def _softmax(x, axis=-1):
    return jax.nn.softmax(x, axis=axis)

def _gelu(x):
    return jax.nn.gelu(x, approximate=True)

def _silu(x):
    return jax.nn.silu(x)

def _sigmoid(x):
    return jax.nn.sigmoid(x)

def _layernorm(x, axis=-1, eps=1e-05):
    m = jnp.mean(x, axis=axis, keepdims=True)
    v = jnp.var(x, axis=axis, keepdims=True)
    return (x - m) / jnp.sqrt(v + eps)

def _scatter_add(tgt, idx, src, axis=0):
    return tgt.at[idx].add(src)

def _segment_sum(src, seg, n):
    return jax.ops.segment_sum(src, seg, n)
kernel_name = 'mk_xattn_ffn_d1_seqx_r4_665f51'

def setup_inputs(seed: int=0):
    np.random.seed(seed)
    _w = jnp.asarray

    def _rec_inputs():
        import jax
        import jax.numpy as jnp
        _rk = jax.random.key(seed)
        x = -0.0003929 + 0.9999 * jax.random.normal(jax.random.fold_in(_rk, 1), (16, 256, 256), jnp.float32)
        _lenS = 256 - jax.random.randint(jax.random.fold_in(_rk, 7), (16,), 0, max(1, 256 // 4) + 1, jnp.int32)
        _lenS2 = 256 - jax.random.randint(jax.random.fold_in(_rk, 8), (16,), 0, max(1, 256 // 4) + 1, jnp.int32)
        _ctx_1024P = jax.random.normal(jax.random.fold_in(_rk, 11), (16, 16, 256), jnp.float32)
        _ctx_1024c = jax.random.dirichlet(jax.random.fold_in(_rk, 511), 0.3 * jnp.ones((16,), jnp.float32), (16, 256))
        _ctx_1024t = jnp.einsum('bsk,bkd->bsd', _ctx_1024c, _ctx_1024P)
        _ctx_1024t = _ctx_1024t * jax.lax.rsqrt(jnp.mean(jnp.square(_ctx_1024t)) + 1e-12) * 0.953939
        ctx_1024 = 2.81802e-05 + 1.00001 * (_ctx_1024t + 0.3 * jax.random.normal(jax.random.fold_in(_rk, 611), (16, 256, 256), jnp.float32))
        return (x, ctx_1024)
    x, ctx_1024 = _rec_inputs()

    def _L0_xattn_setup():
        import jax, jax.numpy as jnp
        import numpy as np
        key = jax.random.key(seed)
        ks = jax.random.split(key, 9)
        B, S, D = (8, 512, 256)
        Qd = Kd = Vd = 256
        s = 1.0 / np.sqrt(D)
        return {'query': jax.random.normal(ks[0], (B, S, D), jnp.float32), 'key': jax.random.normal(ks[1], (B, S, D), jnp.float32), 'value': jax.random.normal(ks[2], (B, S, D), jnp.float32), 'Wq': jax.random.normal(ks[3], (D, Qd), jnp.float32) * s, 'bq': jnp.zeros((Qd,), jnp.float32), 'Wk': jax.random.normal(ks[4], (D, Kd), jnp.float32) * s, 'bk': jnp.zeros((Kd,), jnp.float32), 'Wv': jax.random.normal(ks[5], (D, Vd), jnp.float32) * s, 'bv': jnp.zeros((Vd,), jnp.float32)}
    _L0_xattn_all = _L0_xattn_setup()
    _L0_xattn_in = {k: v for k, v in _L0_xattn_all.items() if k in ('Wq', 'bq', 'Wk', 'bk', 'Wv', 'bv')}
    del _L0_xattn_all

    def _L0_ffn_setup():
        import jax, jax.numpy as jnp
        import numpy as np
        B, L, H, E, FF, C = (4, 512, 256, 8, 1024, 2)
        key = jax.random.key(seed)
        ks = jax.random.split(key, 6)
        s = 0.02
        return {'x': jax.random.normal(ks[0], (B, L, H), dtype=jnp.float32), 'Wg': jax.random.normal(ks[1], (H, E), dtype=jnp.float32) * s, 'W1': jax.random.normal(ks[2], (E, H, FF), dtype=jnp.float32) * s, 'b1': jnp.zeros((E, FF), dtype=jnp.float32), 'W2': jax.random.normal(ks[3], (E, FF, H), dtype=jnp.float32) * s, 'b2': jnp.zeros((E, H), dtype=jnp.float32)}
    _L0_ffn_all = _L0_ffn_setup()
    _L0_ffn_in = {k: v for k, v in _L0_ffn_all.items() if k in ('Wg', 'W1', 'b1', 'W2', 'b2')}
    del _L0_ffn_all
    return {'x': x, 'ctx_1024': ctx_1024, 'L0_xattn_Wq': _L0_xattn_in['Wq'], 'L0_xattn_bq': _L0_xattn_in['bq'], 'L0_xattn_Wk': _L0_xattn_in['Wk'], 'L0_xattn_bk': _L0_xattn_in['bk'], 'L0_xattn_Wv': _L0_xattn_in['Wv'], 'L0_xattn_bv': _L0_xattn_in['bv'], 'L0_ffn_Wg': _L0_ffn_in['Wg'], 'L0_ffn_W1': _L0_ffn_in['W1'], 'L0_ffn_b1': _L0_ffn_in['b1'], 'L0_ffn_W2': _L0_ffn_in['W2'], 'L0_ffn_b2': _L0_ffn_in['b2']}

def reference(x, ctx_1024, L0_xattn_Wq, L0_xattn_bq, L0_xattn_Wk, L0_xattn_bk, L0_xattn_Wv, L0_xattn_bv, L0_ffn_Wg, L0_ffn_W1, L0_ffn_b1, L0_ffn_W2, L0_ffn_b2):
    import jax
    import jax.numpy as jnp

    def _L0_xattn_ref(query, key, value, Wq, bq, Wk, bk, Wv, bv):
        import jax, jax.numpy as jnp
        import numpy as np
        Q = jnp.einsum('bsd,de->bse', query, Wq) + bq
        K = jnp.einsum('bsd,de->bse', key, Wk) + bk
        V = jnp.einsum('bsd,de->bse', value, Wv) + bv
        scale = 1.0 / jnp.sqrt(jnp.asarray(K.shape[-1], Q.dtype))
        scores = jnp.einsum('bqe,bke->bqk', Q, K) * scale
        attn = jax.nn.softmax(scores, axis=-1)
        return jnp.einsum('bqk,bkv->bqv', attn, V)

    def _L0_ffn_ref(x, Wg, W1, b1, W2, b2):
        import jax, jax.numpy as jnp
        import numpy as np
        B, L, H, E, FF, C = (4, 512, 256, 8, 1024, 2)
        b, l, h = x.shape
        e = Wg.shape[1]
        n = b * l
        k = min(max(int(n * C / e), 1), n)
        xt = x.reshape(n, h)
        S = jax.nn.sigmoid(xt @ Wg).T
        G, I = jax.lax.top_k(S, k)
        ex = xt[I]
        hid = jax.nn.gelu(jnp.einsum('ekh,ehf->ekf', ex, W1) + b1[:, None, :], approximate=False)
        out = (jnp.einsum('ekf,efh->ekh', hid, W2) + b2[:, None, :]) * G[..., None]
        new_x = jnp.zeros_like(xt).at[I.reshape(-1)].add(out.reshape(-1, h))
        return new_x.reshape(b, l, h)
    x = x + _L0_xattn_ref(_layernorm(x, axis=-1), ctx_1024, ctx_1024, L0_xattn_Wq, L0_xattn_bq, L0_xattn_Wk, L0_xattn_bk, L0_xattn_Wv, L0_xattn_bv)
    x = x + _L0_ffn_ref(_layernorm(x, axis=-1), L0_ffn_Wg, L0_ffn_W1, L0_ffn_b1, L0_ffn_W2, L0_ffn_b2)
    return x

_drawn_inputs = setup_inputs


def setup_inputs(seed=0):
    import zlib

    import numpy as np

    out = dict(_drawn_inputs(seed))
    spreads = {'L0_xattn_bq': (0.0, 0.319),
     'L0_xattn_bk': (0.0, 0.8),
     'L0_xattn_bv': (0.0, 0.1),
     'L0_ffn_b1': (0.0, 0.286),
     'L0_ffn_b2': (0.0, 0.1)}
    factors = {}
    for name, (base, spread) in spreads.items():
        noise = np.random.default_rng([zlib.crc32(name.encode()), seed]).standard_normal(out[name].shape)
        drawn = base * np.exp(spread * noise) if base else spread * noise
        out[name] = jnp.asarray(drawn.astype(out[name].dtype))
    for name, factor in factors.items():
        out[name] = (out[name] * factor).astype(out[name].dtype)
    return out
```

```python
import math
from contextlib import ExitStack

import numpy as np
import concourse.bass as bass
from concourse import mybir

F32 = mybir.dt.float32
F16 = mybir.dt.float16
BF16 = mybir.dt.bfloat16
I32 = mybir.dt.int32
ALU = mybir.AluOpType
ACT = mybir.ActivationFunctionType
AX = mybir.AxisListType

P = 128


def build(nc, x_d, ctx_d, wq_d, bq_d, wk_d, bk_d, wv_d, bv_d, wg_d, w1_d, b1_d, w2_d, b2_d, out_d):
    B, S, D = x_d.shape
    E, _, FF = w1_d.shape
    N = B * S
    K = max(N * 2 // E, 1)
    NT = N // P
    TP = 4
    NP = NT // TP
    PT_ = TP * P
    DC = D // P
    FC = FF // P
    KT = K // P
    SC = S // P
    EPS = 1e-5

    XS = 4.0
    AS = 16.0
    QS = XS * AS
    PS = 4096.0
    FS = 256.0
    SCORE = 1.0 / (QS * QS * math.sqrt(D))
    BITS = 30
    ROUNDS = BITS // 2
    NOWHERE = float(N)

    with ExitStack() as stack:
        def sb(name, shape, dt=F32):
            return stack.enter_context(nc.sbuf_tensor(name, shape, dt))

        def sem(name):
            return stack.enter_context(nc.semaphore(name))

        rows_d = nc.dram_tensor("rows_d", [N, D], F32).ap()
        gates_d = nc.dram_tensor("gates_d", [N, E], F32).ap()

        ident = sb("ident", [P, P])
        ones16 = sb("ones16", [P, P], BF16)
        before16 = sb("before16", [P, P], BF16)
        same16 = sb("same16", [P, P], BF16)
        apart = sb("apart", [P, P], I32)
        onesf = sb("onesf", [P, P])
        pick = sb("pick", [P, E])
        iota16 = sb("iota16", [P, P], BF16)
        iota8 = sb("iota8", [P, NT, KT])
        tileno = sb("tileno", [P, NT, KT])
        partno = sb("partno", [P, 1])
        mhalf = sb("mhalf", [P, TP])
        eps = sb("eps", [P, TP]); minus = sb("minus", [P, TP])
        dve_tick = sb("dve_tick", [P, 1]); pool_tick = sb("pool_tick", [P, KT + 1])
        w_raw = sb("w_raw", [P, 3, DC, D])
        w_hi = sb("w_hi", [P, 3, DC, D], F16)
        w_lo = sb("w_lo", [P, 3, DC, D], F16)
        wg = sb("wg", [P, DC, E])
        NB1 = E * FC
        brow = sb("brow", [NB1 + 2 * DC, P])
        bcol = sb("bcol", [P, NB1 + 2 * DC])
        bqk = sb("bqk", [P, 2 * DC])
        bv_bc = sb("bv_bc", [P, TP, D])
        b2_bc = sb("b2_bc", [P, E, D])
        xres = sb("xres", [P, NT, D])
        ctx = sb("ctx", [P, TP, D])
        xn = sb("xn", [P, TP, D])
        xn2 = sb("xn2", [P, TP, D])
        st1 = sb("st1", [P, TP, 6]); mv1 = sb("mv1", [P, TP, 2])
        rstd1 = sb("rstd1", [P, TP]); nmr1 = sb("nmr1", [P, TP])
        st2 = sb("st2", [P, TP, 6]); mv2 = sb("mv2", [P, TP, 2])
        rstd2 = sb("rstd2", [P, TP]); nmr2 = sb("nmr2", [P, TP])
        xT = [sb(f"xT{i}", [P, DC, PT_], F16) for i in "hl"]
        cT = [sb(f"cT{i}", [P, DC, PT_], F16) for i in "hl"]
        qT = [sb(f"qT{i}", [P, DC, PT_], F16) for i in "hl"]
        kT = [sb(f"kT{i}", [P, DC, PT_], F16) for i in "hl"]
        v = [sb(f"v{i}", [P, TP, D], F16) for i in "hl"]
        prob = sb("prob", [P, TP, S])
        pT = [sb(f"pT{i}", [P, SC, PT_], F16) for i in "hl"]
        nmax = sb("nmax", [P, TP]); nbias = sb("nbias", [P, TP])
        rsum = sb("rsum", [P, TP]); rinv = sb("rinv", [P, TP]); rinvs = sb("rinvs", [P, TP])
        xn2T = sb("xn2T", [P, DC, PT_])
        logit = sb("logit", [P, NT, E])
        gate = sb("gate", [P, NT, E])
        HT = NT // 2
        keyT = sb("keyT", [P, 2, P])
        junk = sb("junk", [P, 3, 2, P], BF16)
        steps = sb("steps", [P, 3], I32)
        found = sb("found", [P, 3], I32)
        gain = sb("gain", [P, 1], I32)
        base = sb("base", [P, 1], I32)
        trial = sb("trial", [P, 3], I32)
        cnt = sb("cnt", [P, 3], BF16)
        kth_q = sb("kth_q", [P, E])
        kth = sb("kth", [P, E])
        above = sb("above", [P, 2, NT, E], BF16)
        run = [sb(f"run{i}", [P, 2, NT + 1, E]) for i in range(2)]
        place = sb("place", [P, 2, NT, E])
        pos = sb("pos", [P, NT, E], I32)
        loi = sb("loi", [P, NT, E], I32); hii = sb("hii", [P, NT, E], I32)
        lof = sb("lof", [P, NT, E]); hif = sb("hif", [P, NT, E])
        lo_e = sb("lo_e", [P, NT])
        oneh = sb("oneh", [P, NT, P], BF16)
        inhi = sb("inhi", [P, NT, KT])
        val = sb("val", [P, NT, 2, KT], BF16)
        idp = sb("idp", [P, 2, KT])
        ids = sb("ids", [P, KT], I32)
        ids_s = sb("ids_s", [P, KT], I32)
        ex = sb("ex", [P, KT, D])
        gex = sb("gex", [P, KT, E])
        ge = sb("ge", [P, KT])
        exT = [sb(f"exT{i}", [P, DC, K], F16) for i in "hl"]
        w1r = sb("w1r", [P, DC, FF]); w2r = sb("w2r", [P, FC, D])
        w1 = [sb(f"w1{i}", [P, DC, FF], F16) for i in "hl"]
        w2 = [sb(f"w2{i}", [P, FC, D], F16) for i in "hl"]
        b1e = sb("b1e", [P, FC])
        b2e = sb("b2e", [P, D])
        g32 = sb("g32", [P, 2, PT_])
        hid = [xres[:, i * NT // 2:(i + 1) * NT // 2, :].bitcast(F16).rearrange("p t d -> p (t d)")
               .rearrange("p (f k) -> p f k", f=FC) for i in range(2)]
        yt = sb("yt", [P, 2, D])
        yo = sb("yo", [P, KT, D])

        bank = [stack.enter_context(nc.psum_tensor(f"bank{i}", [P, 2, 512], F32)) for i in range(4)]
        A_, B_, C_, D_ = bank

        names = """ld_x0 ld_x1 ld_w ld_wg ld_b ld_bv ld_b2 ld_ctx const0 const1 const2 and_s same_s
            w_hi_s w_lo_s b_tr b_col b_qk
            ln1_st ln1_mv ln1_eps ln1_rstd ln1_mr ln1_nmr xn_rdy xbv
            x_tr x_hi x_lo c_tr c_hi c_lo q_mm q_hi q_lo k_mm k_hi k_lo v_mm v_hi v_lo
            s_mm s_max s_nb s_exp s_ri s_ris p_tr p_hi p_lo o_mm o_ev
            ln2_st ln2_mv ln2_eps ln2_rstd ln2_mr ln2_nmr xn2_rdy st_x1 st_xn
            x2_tr x2_ev l_mm l_ev
            gate_r st_gate key_tr key_ev init_s srch_tr srch_cmp srch_mm srch_sel srch_red srch_base srch_step
            kq_s kq_mm kth_s above_s pref_mm tot_mm run_s place_s pos_a pos_s split_i split_f
            lo_s hot_s hi_s val_s id_mm id_ev ids_s_ idss_s gat gatg ge_s ex_tr ex_hi ex_lo
            ld_w1 ld_w2 w1_hi_s w1_lo_s w2_hi_s w2_lo_s b1e_s b2e_s
            h_mm h_g h_hi h_lo y_mm y_t y_o sc_done tick_g tick_s""".split()
        s = {n: sem(n) for n in names}

        block = stack.enter_context(nc.Block())
        MID0, MID1 = 3, NP - 3

        def phase_a(engine, body):
            for n in range(MID0):
                body(n, n)
            with engine.Fori(MID0, MID1 + 1) as n:
                body(n, None)
            for n in range(MID1 + 1, NP + 2):
                body(n, n)

        def runs(n, k, shift):
            return k is None or 0 <= k - shift < NP

        def tiles(n):
            return bass.ds(n * TP, TP)

        @block.sync
        def _(sp):
            xv = x_d.rearrange("b (c p) d -> p (b c) d", p=P)
            cv = ctx_d.rearrange("b (c p) d -> p (b c) d", p=P)
            ov = out_d.rearrange("b (c p) d -> p (b c) d", p=P)
            rv = rows_d.rearrange("(t p) d -> p t d", p=P)
            sp.dma_start(xres[:, 0:TP, :], xv[:, 0:TP, :]).then_inc(s["ld_x0"], 16)
            sp.dma_start(ctx[:, :, :], cv[:, 0:TP, :]).then_inc(s["ld_ctx"], 16)
            for i, w_d in enumerate((wq_d, wk_d, wv_d)):
                sp.dma_start(w_raw[:, i], w_d.rearrange("(c p) e -> p c e", p=P)).then_inc(s["ld_w"], 16)
            sp.dma_start(brow[0:NB1, :], b1_d.rearrange("e (f p) -> (e f) p", p=P)).then_inc(s["ld_b"], 16)
            sp.dma_start(brow[NB1:NB1 + DC, :], bq_d.rearrange("(f p) -> f p", p=P)).then_inc(s["ld_b"], 16)
            sp.dma_start(brow[NB1 + DC:NB1 + 2 * DC, :], bk_d.rearrange("(f p) -> f p", p=P)).then_inc(s["ld_b"], 16)
            sp.dma_start(xres[:, TP:NT, :], xv[:, TP:NT, :]).then_inc(s["ld_x1"], 16)
            sp.dma_start(wg[:, :, :], wg_d.rearrange("(c p) e -> p c e", p=P)).then_inc(s["ld_wg"], 16)
            for t in range(TP):
                sp.dma_start(bv_bc[:, t, :], bv_d.partition_broadcast(P)).then_inc(s["ld_bv"], 16)
            for e in range(E):
                sp.dma_start(b2_bc[:, e, :], b2_d[e, :].partition_broadcast(P)).then_inc(s["ld_b2"], 16)
            sp.dma_start(w1r[:, :, :], w1_d[0].rearrange("(c p) f -> p c f", p=P)).then_inc(s["ld_w1"], 16)
            sp.dma_start(w2r[:, :, :], w2_d[0].rearrange("(c p) f -> p c f", p=P)).then_inc(s["ld_w2"], 16)

            def body(n, k):
                if runs(n, k, -1):
                    sp.wait_ge(s["c_tr"], n + 1)
                    sp.dma_start(ctx[:, :, :], cv[:, tiles(n + 1), :]).then_inc(s["ld_ctx"], 16)
                if runs(n, k, 1):
                    sp.wait_ge(s["o_ev"], TP * n)
                    sp.dma_start(ov[:, tiles(n - 1), :], xres[:, tiles(n - 1), :]).then_inc(s["st_x1"], 16)
                    sp.wait_ge(s["xn2_rdy"], TP * n)
                    sp.dma_start(rv[:, tiles(n - 1), :], xn2[:, :, :]).then_inc(s["st_xn"], 16)

            phase_a(sp, body)
            sp.wait_ge(s["gate_r"], 1)
            sp.dma_start(gates_d.rearrange("(t p) e -> p t e", p=P), gate[:, :, :]).then_inc(s["st_gate"], 16)
            with sp.Fori(1, E) as e:
                sp.wait_ge(s["w1_lo_s"], 4 * e)
                sp.dma_start(w1r[:, :, :], w1_d[bass.ds(e, 1)].rearrange("o (c p) f -> p (o c) f", p=P)).then_inc(s["ld_w1"], 16)
                sp.wait_ge(s["w2_lo_s"], 4 * e)
                sp.dma_start(w2r[:, :, :], w2_d[bass.ds(e, 1)].rearrange("o (c p) f -> p (o c) f", p=P)).then_inc(s["ld_w2"], 16)
            sp.wait_ge(s["sc_done"], 16 * KT * E)
            sp.wait_ge(s["st_x1"], 16 * NP)
            sp.wait_ge(s["st_xn"], 16 * NP)
            sp.wait_ge(s["st_gate"], 16)

        @block.gpsimd
        def _(pool):
            pool.memset(ident[:], 0.0).then_inc(s["const0"], 1)
            pool.memset(before16[:], 1.0).then_inc(s["const0"], 1)
            pool.memset(pick[:], 0.0).then_inc(s["const0"], 1)
            pool.wait_ge(s["const0"], 3)
            pool.affine_select(out=ident[:], in_=ident[:], compare_op=ALU.not_equal, fill=1.0, base=0,
                               pattern=[[-1, P]], channel_multiplier=1).then_inc(s["const1"], 1)
            pool.affine_select(out=before16[:], in_=before16[:], compare_op=ALU.is_gt, fill=0.0, base=0,
                               pattern=[[1, P]], channel_multiplier=-1).then_inc(s["const1"], 1)
            pool.affine_select(out=pick[:], in_=pick[:], compare_op=ALU.not_equal, fill=1.0, base=0,
                               pattern=[[-1, E]], channel_multiplier=1).then_inc(s["const1"], 1)
            pool.memset(mhalf[:], -0.5).then_inc(s["const1"], 1)
            pool.memset(eps[:], EPS).then_inc(s["const1"], 1)
            pool.memset(minus[:], -1.0).then_inc(s["const1"], 1)
            pool.memset(ones16[:], 1.0).then_inc(s["const1"], 1)
            pool.memset(onesf[:], 1.0).then_inc(s["const1"], 1)

            def ln_scale(mv, rstd, nmr, a, n):
                pool.tensor_tensor(rstd[:], mv[:, :, 1], eps[:], ALU.add).then_inc(s[a + "_eps"], 1)
                pool.wait_ge(s[a + "_eps"], n + 1)
                pool.tensor_tensor(rstd[:], rstd[:], mhalf[:], ALU.pow).then_inc(s[a + "_rstd"], 1)
                pool.wait_ge(s[a + "_rstd"], n + 1)
                pool.tensor_tensor(nmr[:], mv[:, :, 0], rstd[:], ALU.mult).then_inc(s[a + "_mr"], 1)
                pool.wait_ge(s[a + "_mr"], n + 1)
                pool.tensor_tensor(nmr[:], nmr[:], minus[:], ALU.mult).then_inc(s[a + "_nmr"], 1)

            def ln1(n, first=False):
                pool.wait_ge(s["ln1_mv"], TP * (n + 1))
                if not first:
                    pool.wait_ge(s["xn_rdy"], TP * n)
                ln_scale(mv1, rstd1, nmr1, "ln1", n)

            def add_bv(n):
                pool.wait_ge(s["xn_rdy"], TP * (n + 1))
                pool.tensor_tensor(xres[:, tiles(n), :], xres[:, tiles(n), :], bv_bc[:], ALU.add).then_inc(s["xbv"], 1)

            pool.wait_ge(s["const1"], 6)
            ln1(0, True)
            pool.iota(apart[:], [[1, P]], base=P, channel_multiplier=-1).then_inc(s["const2"], 1)
            pool.iota(iota16[:], [[1, P]], base=0, channel_multiplier=0, allow_small_or_imprecise_dtypes=True).then_inc(s["const2"], 1)
            pool.iota(iota8[:], [[0, NT], [1, KT]], base=0, channel_multiplier=0, allow_small_or_imprecise_dtypes=True).then_inc(s["const2"], 1)
            pool.iota(tileno[:], [[1, NT], [0, KT]], base=0, channel_multiplier=0, allow_small_or_imprecise_dtypes=True).then_inc(s["const2"], 1)
            pool.iota(partno[:], [[0, 1]], base=0, channel_multiplier=1, allow_small_or_imprecise_dtypes=True).then_inc(s["const2"], 1)
            pool.wait_ge(s["ld_bv"], 16 * TP)
            add_bv(0)
            ln1(1)

            def body(n, k):
                if runs(n, k, -1):
                    add_bv(n + 1)
                if runs(n, k, 1):
                    pool.wait_ge(s["ln2_mv"], TP * n)
                    if k != 1:
                        pool.wait_ge(s["xn2_rdy"], TP * (n - 1))
                    ln_scale(mv2, rstd2, nmr2, "ln2", n - 1)
                if runs(n, k, -2):
                    ln1(n + 2)

            phase_a(pool, body)

            rows_out = out_d.rearrange("b s d -> (b s) d")

            def gather(e, first):
                pool.wait_ge(s["ids_s_"], e + 1)
                if not first:
                    pool.wait_ge(s["ex_tr"], 4 * e)
                    pool.wait_ge(s["ge_s"], e)
                if not first:
                    pool.wait_ge(s["tick_g"], e)
                pool.tensor_tensor(pool_tick[:, 0:1], eps[:, 0:1], eps[:, 0:1], ALU.add).then_inc(s["tick_g"], 1)
                for t in range(KT):
                    pool.indirect_dma_start(out=ex[:, t, :], out_offset=None, in_=rows_d,
                                            in_offset=bass.IndirectOffsetOnAxis(ap=ids[:, t:t + 1], axis=0)).then_inc(s["gat"], 16)
                for t in range(KT):
                    pool.indirect_dma_start(out=gex[:, t, :], out_offset=None, in_=gates_d,
                                            in_offset=bass.IndirectOffsetOnAxis(ap=ids[:, t:t + 1], axis=0)).then_inc(s["gatg"], 16)

            def scatter(e, first):
                if not first:
                    pool.wait_ge(s["sc_done"], 16 * KT * e)
                for t in range(KT):
                    pool.wait_ge(s["y_o"], KT * e + t + 1)
                    if not first:
                        pool.wait_ge(s["tick_s"], KT * (e - 1) + t + 1)
                    pool.tensor_tensor(pool_tick[:, t + 1:t + 2], eps[:, 0:1], eps[:, 0:1], ALU.add).then_inc(s["tick_s"], 1)
                    pool.indirect_dma_start(out=rows_out, out_offset=bass.IndirectOffsetOnAxis(ap=ids_s[:, t:t + 1], axis=0),
                                            in_=yo[:, t, :], in_offset=None, compute_op=ALU.add).then_inc(s["sc_done"], 16)

            pool.wait_ge(s["st_xn"], 16 * NP)
            pool.wait_ge(s["st_gate"], 16)
            gather(0, True)
            pool.wait_ge(s["st_x1"], 16 * NP)
            gather(1, False)
            scatter(0, True)
            with pool.Fori(1, E - 1) as e:
                gather(e + 1, False)
                scatter(e, False)
            scatter(E - 1, False)

        @block.scalar
        def _(act):
            def hi(dst, src, mm, done, count, scale=1.0, bias=0.0, func=ACT.Identity):
                act.wait_ge(s[mm], count)
                act.activation(dst, src, func, bias=bias, scale=scale).then_inc(s[done], 1)

            def apply_ln(dst, rstd, nmr, a, n, done):
                act.wait_ge(s[a + "_nmr"], n + 1)
                for t in range(TP):
                    act.activation(dst[:, t, :], xres[:, bass.ds(n * TP + t, 1), :].rearrange("p o d -> p (o d)"), ACT.Identity,
                                   bias=nmr[:, t:t + 1], scale=rstd[:, t:t + 1]).then_inc(s[done], 1)

            apply_ln(xn, rstd1, nmr1, "ln1", 0, "xn_rdy")
            act.wait_ge(s["ld_w"], 48)
            act.activation(w_hi[:], w_raw[:], ACT.Copy, scale=AS).then_inc(s["w_hi_s"], 1)
            act.wait_ge(s["b_tr"], 1)
            act.activation(bcol[:], D_[:, 1, 0:NB1 + 2 * DC], ACT.Copy).then_inc(s["b_col"], 1)
            hi(xT[0][:], B_[:], "x_tr", "x_hi", 1, scale=XS)
            hi(cT[0][:], C_[:], "c_tr", "c_hi", 1, scale=XS)
            apply_ln(xn, rstd1, nmr1, "ln1", 1, "xn_rdy")
            act.wait_ge(s["b_qk"], 1)

            def body(n, k):
                if runs(n, k, 0):
                    act.wait_ge(s["q_mm"], n + 1)
                    if k != 0:
                        act.wait_ge(s["s_mm"], n)
                    for c in range(DC):
                        act.activation(qT[0][:, c, :], A_[:, c, :], ACT.Identity, bias=bqk[:, c:c + 1]).then_inc(s["q_hi"], 1)
                    act.wait_ge(s["k_mm"], n + 1)
                    for c in range(DC):
                        act.activation(kT[0][:, c, :], D_[:, c, :], ACT.Identity, bias=bqk[:, DC + c:DC + c + 1]).then_inc(s["k_hi"], 1)
                if runs(n, k, 1):
                    if k != 1:
                        act.wait_ge(s["o_mm"], n - 1)
                    hi(pT[0][:], B_[:], "p_tr", "p_hi", n)
                if runs(n, k, 0):
                    act.wait_ge(s["v_mm"], n + 1)
                    if k != 0:
                        act.wait_ge(s["o_mm"], n)
                    act.activation(v[0][:], A_[:].rearrange("p a (b d) -> p (a b) d", d=D), ACT.Identity).then_inc(s["v_hi"], 1)
                if runs(n, k, -1):
                    hi(xT[0][:], D_[:], "x_tr", "x_hi", n + 2, scale=XS)
                    hi(cT[0][:], C_[:], "c_tr", "c_hi", n + 2, scale=XS)
                if runs(n, k, 0):
                    act.wait_ge(s["s_nb"], n + 1)
                    if k != 0:
                        act.wait_ge(s["p_tr"], n)
                        act.wait_ge(s["s_ri"], n)
                    for t in range(TP):
                        act.activation(prob[:, t, :], B_[:, t // 2, (t % 2) * S:(t % 2 + 1) * S], ACT.Exp,
                                       bias=nbias[:, t:t + 1], scale=SCORE,
                                       accum_out=rsum[:, t:t + 1]).then_inc(s["s_exp"], 1)
                if runs(n, k, 1):
                    if k != 1:
                        act.wait_ge(s["x2_tr"], n - 1)
                        act.wait_ge(s["st_xn"], 16 * (n - 1))
                    apply_ln(xn2, rstd2, nmr2, "ln2", n - 1, "xn2_rdy")
                if runs(n, k, -2):
                    act.wait_ge(s["x_tr"], n + 2)
                    apply_ln(xn, rstd1, nmr1, "ln1", n + 2, "xn_rdy")

            phase_a(act, body)
            act.wait_ge(s["l_ev"], NP)
            act.activation(gate[:], logit[:], ACT.Sigmoid).then_inc(s["gate_r"], 1)
            act.wait_ge(s["key_tr"], 1)
            act.activation(keyT[:], A_[:, 0, 0:2 * P].rearrange("p (a b) -> p a b", a=2), ACT.Copy).then_inc(s["key_ev"], 1)

            def w1_hi(e, c):
                act.activation(w1[0][:, c], w1r[:, c], ACT.Copy, scale=FS).then_inc(s["w1_hi_s"], 1)

            def ex_hi(e, i):
                act.wait_ge(s["ex_tr"], 4 * e + i + 1)
                act.activation(exT[0][:, i % 2, (i // 2) * 512:(i // 2 + 1) * 512], D_[:, i % 2, :],
                               ACT.Copy, scale=XS).then_inc(s["ex_hi"], 1)

            def layer1(e, first):
                act.wait_ge(s["b1e_s"], e + 1)
                for u in range(2 * FC):
                    h, f = u // FC, u % FC
                    act.wait_ge(s["h_mm"], 2 * FC * e + u + 1)
                    src = bank[(u % 4) // 2][:, u % 2, :]
                    if not (first and u < 2):
                        act.wait_ge(s["h_lo"], 2 * FC * e + u - 1)
                    act.activation(g32[:, u % 2, :], src, ACT.Gelu, bias=b1e[:, f:f + 1],
                                   scale=1.0 / (XS * FS)).then_inc(s["h_g"], 1)
                    if not first and f == 0:
                        act.wait_ge(s["y_mm"], KT * (e - 1) + (KT // 2) * (h + 1))
                    act.activation(hid[0][:, f, h * 512:(h + 1) * 512], src, ACT.Gelu, bias=b1e[:, f:f + 1],
                                   scale=1.0 / (XS * FS)).then_inc(s["h_hi"], 1)

            def layer2(e, first, last):
                act.wait_ge(s["ge_s"], e + 1)
                if not first:
                    act.wait_ge(s["sc_done"], 16 * KT * e)
                if not last:
                    act.wait_ge(s["ld_w1"], 16 * (e + 2))
                for t in range(KT):
                    if not last and t < DC:
                        w1_hi(e + 1, t)
                    if not last and t >= KT - 4:
                        ex_hi(e + 1, t - (KT - 4))
                    act.wait_ge(s["y_t"], KT * e + t + 1)
                    act.activation(yo[:, t, :], yt[:, t % 2, :], ACT.Copy, scale=ge[:, t:t + 1]).then_inc(s["y_o"], 1)

            act.wait_ge(s["ld_w1"], 16)
            for c in range(DC):
                w1_hi(0, c)
            for i in range(4):
                ex_hi(0, i)
            act.wait_ge(s["st_x1"], 16 * NP)
            layer1(0, True)
            layer2(0, True, False)
            with act.Fori(1, E - 1) as e:
                layer1(e, False)
                layer2(e, False, False)
            layer1(E - 1, False)
            layer2(E - 1, False, True)

        @block.vector
        def _(dve):
            def stats(n, st, mv, a, src_ready, need):
                if src_ready is not None:
                    dve.wait_ge(s[src_ready], need)
                dve.memset(dve_tick[:], 0.0)
                for t in range(TP):
                    dve.bn_stats(st[:, t, :], xres[:, bass.ds(n * TP + t, 1), :].rearrange("p o d -> p (o d)")).then_inc(s[a + "_st"], 1)
                dve.wait_ge(s[a + "_st"], TP * (n + 1))
                dve.memset(dve_tick[:], 0.0)
                for t in range(TP):
                    dve.bn_aggr(mv[:, t, :], st[:, t, :]).then_inc(s[a + "_mv"], 1)

            def lo(dst, src, hi_, ready, count, done, scale=None):
                dve.wait_ge(s[ready], count)
                if scale is None:
                    dve.tensor_tensor(dst, src, hi_, ALU.subtract).then_inc(s[done], 1)
                else:
                    dve.scalar_tensor_tensor(dst, src, scale, hi_, ALU.mult, ALU.subtract).then_inc(s[done], 1)

            dve.wait_ge(s["ld_x0"], 16)
            stats(0, st1, mv1, "ln1", None, 0)
            lo(w_lo[:].rearrange("p a b c -> p (a b c)"), w_raw[:].rearrange("p a b c -> p (a b c)"), w_hi[:].rearrange("p a b c -> p (a b c)"), "w_hi_s", 1, "w_lo_s", AS)
            dve.wait_ge(s["b_col"], 1)
            dve.tensor_scalar(bqk[:], bcol[:, NB1:], QS, None, ALU.mult).then_inc(s["b_qk"], 1)
            dve.wait_ge(s["b_qk"], 1)
            lo(xT[1][:], B_[:], xT[0][:], "x_hi", 1, "x_lo", XS)
            lo(cT[1][:], C_[:], cT[0][:], "c_hi", 1, "c_lo", XS)
            dve.wait_ge(s["ld_x1"], 16)
            dve.wait_ge(s["ln1_nmr"], 1)
            stats(1, st1, mv1, "ln1", None, 0)

            def body(n, k):
                if runs(n, k, 0):
                    for c in range(DC):
                        dve.wait_ge(s["q_hi"], DC * n + c + 1)
                        dve.scalar_tensor_tensor(qT[1][:, c, :], A_[:, c, :], bqk[:, c:c + 1], qT[0][:, c, :], ALU.add, ALU.subtract).then_inc(s["q_lo"], 1)
                if runs(n, k, 2):
                    dve.wait_ge(s["x2_tr"], n - 1)
                    if k != 2:
                        dve.wait_ge(s["l_mm"], n - 2)
                    dve.tensor_copy(xn2T[:], C_[:]).then_inc(s["x2_ev"], 1)
                if runs(n, k, 0):
                    for c in range(DC):
                        dve.wait_ge(s["k_hi"], DC * n + c + 1)
                        dve.scalar_tensor_tensor(kT[1][:, c, :], D_[:, c, :], bqk[:, DC + c:DC + c + 1], kT[0][:, c, :], ALU.add, ALU.subtract).then_inc(s["k_lo"], 1)
                if runs(n, k, 1):
                    lo(pT[1][:], B_[:], pT[0][:], "p_hi", n, "p_lo")
                if runs(n, k, 2):
                    dve.wait_ge(s["l_mm"], n - 1)
                    dve.tensor_copy(logit[:, tiles(n - 2), :], C_[:, 0, 0:TP * E].rearrange("p (t e) -> p t e", e=E)).then_inc(s["l_ev"], 1)
                if runs(n, k, 1):
                    dve.wait_ge(s["xbv"], n)
                    dve.wait_ge(s["s_ris"], n)
                    for t in range(TP):
                        dve.wait_ge(s["o_mm"], n)
                        xt = xres[:, bass.ds((n - 1) * TP + t, 1), :].rearrange("p o d -> p (o d)")
                        dve.scalar_tensor_tensor(xt, B_[:, t // 2, (t % 2) * D:(t % 2 + 1) * D], rinvs[:, t:t + 1], xt,
                                                 ALU.mult, ALU.add).then_inc(s["o_ev"], 1)
                if runs(n, k, 0):
                    lo(v[1][:], A_[:].rearrange("p a (b d) -> p (a b) d", d=D), v[0][:], "v_hi", n + 1, "v_lo")
                if runs(n, k, 1):
                    if k != 1:
                        dve.wait_ge(s["ln2_nmr"], n - 1)
                    stats(n - 1, st2, mv2, "ln2", "o_ev", TP * n)
                if runs(n, k, -1):
                    lo(xT[1][:], D_[:], xT[0][:], "x_hi", n + 2, "x_lo", XS)
                    lo(cT[1][:], C_[:], cT[0][:], "c_hi", n + 2, "c_lo", XS)
                if runs(n, k, 0):
                    dve.wait_ge(s["s_mm"], n + 1)
                    dve.tensor_reduce(nmax[:], B_[:].rearrange("p a (b k) -> p (a b) k", k=S), AX.X, ALU.max, negate=True).then_inc(s["s_max"], 1)
                    if k != 0:
                        dve.wait_ge(s["s_exp"], TP * n)
                    dve.wait_ge(s["s_max"], n + 1)
                    dve.tensor_scalar(nbias[:], nmax[:], SCORE, math.log(PS), ALU.mult, ALU.add).then_inc(s["s_nb"], 1)
                if runs(n, k, -2):
                    dve.wait_ge(s["ln1_nmr"], n + 2)
                    stats(n + 2, st1, mv1, "ln1", None, 0)
                if runs(n, k, 0):
                    dve.wait_ge(s["s_exp"], TP * (n + 1))
                    dve.reciprocal(rinv[:], rsum[:]).then_inc(s["s_ri"], 1)
                    dve.wait_ge(s["s_ri"], n + 1)
                    dve.tensor_scalar(rinvs[:], rinv[:], 1.0 / QS, None, ALU.mult).then_inc(s["s_ris"], 1)

            phase_a(dve, body)

            dve.wait_ge(s["const2"], 5)
            dve.tensor_scalar(apart[:], apart[:], E - 1, None, ALU.bitwise_and).then_inc(s["and_s"], 1)
            dve.wait_ge(s["and_s"], 1)
            dve.tensor_scalar(same16[:], apart[:], 0.0, None, ALU.is_equal).then_inc(s["same_s"], 1)
            for c in range(3):
                dve.memset(steps[:, c:c + 1], (c + 1) << (BITS - 2)).then_inc(s["init_s"], 1)
            dve.memset(base[:], 0).then_inc(s["init_s"], 1)
            dve.wait_ge(s["init_s"], 4)
            dve.wait_ge(s["key_ev"], 1)
            with dve.Fori(0, ROUNDS) as r:
                dve.tensor_tensor(trial[:], steps[:], base[:, 0:1].broadcast_to([P, 3]), ALU.bitwise_or).then_inc(s["srch_tr"], 1)
                dve.wait_ge(s["srch_tr"], r + 1)
                for c in range(3):
                    dve.tensor_scalar(junk[:, c], keyT[:], trial[:, c:c + 1].bitcast(F32), None, ALU.is_ge, ALU.add,
                                      accum_out=cnt[:, c:c + 1]).then_inc(s["srch_cmp"], 1)
                dve.wait_ge(s["srch_mm"], r + 1)
                dve.scalar_tensor_tensor(found[:], A_[:, 1, 0:3], float(K), steps[:, 0:1].broadcast_to([P, 3]), ALU.is_ge, ALU.mult).then_inc(s["srch_sel"], 1)
                dve.wait_ge(s["srch_sel"], r + 1)
                with nc.allow_low_precision(reason="a sum of one to three equal powers of two"):
                    dve.tensor_reduce(gain[:], found[:], AX.X, ALU.add).then_inc(s["srch_red"], 1)
                dve.tensor_scalar(steps[:], steps[:], 2, None, ALU.logical_shift_right).then_inc(s["srch_step"], 1)
                dve.wait_ge(s["srch_red"], r + 1)
                dve.tensor_tensor(base[:], base[:], gain[:], ALU.bitwise_or).then_inc(s["srch_base"], 1)
                dve.wait_ge(s["srch_step"], r + 1)
                dve.wait_ge(s["srch_base"], r + 1)
            dve.tensor_scalar(kth_q[:], pick[:], base[:].bitcast(F32), None, ALU.mult).then_inc(s["kq_s"], 1)
            dve.wait_ge(s["kq_mm"], 1)
            dve.tensor_copy(kth[:], A_[:, 0, 0:E]).then_inc(s["kth_s"], 1)
            dve.wait_ge(s["kth_s"], 1)
            kb = kth[:, :].unsqueeze(1).broadcast_to([P, NT, E])
            dve.wait_ge(s["gate_r"], 1)
            dve.tensor_tensor(above[:, 0], gate[:], kb, ALU.is_gt).then_inc(s["above_s"], 1)
            dve.tensor_tensor(above[:, 1], gate[:], kb, ALU.is_equal).then_inc(s["above_s"], 1)
            dve.memset(run[0][:, :, 0, :], 0.0).then_inc(s["run_s"], 1)
            dve.wait_ge(s["tot_mm"], 1)
            dve.tensor_copy(run[0][:, :, 1:, :], C_[:, 0, :].rearrange("p (a t e) -> p a t e", a=2, e=E)).then_inc(s["run_s"], 1)
            dve.wait_ge(s["run_s"], 2)
            now, step, ran = 0, 1, 2
            while step <= NT:
                a, b = run[now], run[1 - now]
                dve.tensor_copy(b[:, :, 0:step, :], a[:, :, 0:step, :]).then_inc(s["run_s"], 1)
                dve.tensor_tensor(b[:, :, step:, :], a[:, :, step:, :], a[:, :, 0:NT + 1 - step, :], ALU.add).then_inc(s["run_s"], 1)
                ran += 2
                dve.wait_ge(s["run_s"], ran)
                now, step = 1 - now, 2 * step
            acc = run[now]
            dve.wait_ge(s["pref_mm"], 1)
            for h in range(2):
                dve.tensor_tensor(place[:, h], B_[:, 0, h * NT * E:(h + 1) * NT * E].rearrange("p (t e) -> p t e", e=E),
                                  acc[:, h, 0:NT, :], ALU.add).then_inc(s["place_s"], 1)
            dve.wait_ge(s["place_s"], 2)
            dve.tensor_tensor(place[:, 1], place[:, 1], acc[:, 0, NT:NT + 1, :].broadcast_to([P, NT, E]), ALU.add).then_inc(s["place_s"], 1)
            dve.wait_ge(s["place_s"], 3)
            for h in range(2):
                dve.scalar_tensor_tensor(place[:, h].rearrange("p t e -> p (t e)"), place[:, h].rearrange("p t e -> p (t e)"), NOWHERE,
                                         above[:, h].rearrange("p t e -> p (t e)"), ALU.subtract, ALU.mult).then_inc(s["pos_a"], 1)
            dve.wait_ge(s["pos_a"], 2)
            dve.scalar_tensor_tensor(pos[:].rearrange("p t e -> p (t e)"), place[:, 0].rearrange("p t e -> p (t e)"), NOWHERE,
                                     place[:, 1].rearrange("p t e -> p (t e)"), ALU.add, ALU.add).then_inc(s["pos_s"], 1)
            dve.wait_ge(s["pos_s"], 1)
            dve.tensor_scalar(loi[:], pos[:], P - 1, None, ALU.bitwise_and).then_inc(s["split_i"], 1)
            dve.tensor_scalar(hii[:], pos[:], int(math.log2(P)), None, ALU.logical_shift_right).then_inc(s["split_i"], 1)
            dve.wait_ge(s["split_i"], 2)
            dve.tensor_copy(lof[:], loi[:]).then_inc(s["split_f"], 1)
            dve.tensor_copy(hif[:], hii[:]).then_inc(s["split_f"], 1)
            dve.wait_ge(s["split_f"], 2)

            def places(e, first):
                if not first:
                    dve.wait_ge(s["id_mm"], e)
                dve.tensor_copy(lo_e[:], lof[:, :, bass.ds(e, 1)].rearrange("p t o -> p (t o)")).then_inc(s["lo_s"], 1)
                dve.tensor_tensor(inhi[:], iota8[:], hif[:, :, bass.ds(e, 1)].broadcast_to([P, NT, KT]), ALU.is_equal).then_inc(s["hi_s"], 1)
                dve.wait_ge(s["hi_s"], e + 1)
                dve.tensor_tensor(val[:, :, 0, :], inhi[:], tileno[:], ALU.mult).then_inc(s["val_s"], 1)
                dve.tensor_scalar(val[:, :, 1, :], inhi[:], partno[:, 0:1], None, ALU.mult).then_inc(s["val_s"], 1)
                dve.wait_ge(s["lo_s"], e + 1)

            def onehot(t0, t1):
                for t in range(t0, t1):
                    dve.tensor_scalar(oneh[:, t, :], iota16[:], lo_e[:, t:t + 1], None, ALU.is_equal).then_inc(s["hot_s"], 1)

            def ids_of(e, first):
                dve.wait_ge(s["id_mm"], e + 1)
                dve.tensor_copy(idp[:], D_[:, 0, 0:2 * KT].rearrange("p (a t) -> p a t", a=2)).then_inc(s["id_ev"], 1)
                dve.wait_ge(s["id_ev"], e + 1)
                if not first:
                    dve.wait_ge(s["gat"], 16 * KT * e)
                    dve.wait_ge(s["gatg"], 16 * KT * e)
                    dve.wait_ge(s["idss_s"], e)
                dve.scalar_tensor_tensor(ids[:], idp[:, 0, :], float(P), idp[:, 1, :], ALU.mult, ALU.add).then_inc(s["ids_s_"], 1)

            def keep(e, first):
                dve.wait_ge(s["gatg"], 16 * KT * (e + 1))
                if not first:
                    dve.wait_ge(s["y_o"], KT * e)
                    dve.wait_ge(s["sc_done"], 16 * KT * e)
                dve.tensor_copy(ge[:], gex[:, :, bass.ds(e, 1)].rearrange("p t o -> p (t o)")).then_inc(s["ge_s"], 1)
                dve.tensor_copy(ids_s[:], ids[:]).then_inc(s["idss_s"], 1)
                dve.tensor_copy(b2e[:], b2_bc[:, bass.ds(e, 1), :].rearrange("p o d -> p (o d)")).then_inc(s["b2e_s"], 1)

            def b1_of(e, first):
                if not first:
                    dve.wait_ge(s["h_hi"], 2 * FC * e)
                dve.tensor_copy(b1e[:], bcol[:, bass.ds(e * FC, FC)]).then_inc(s["b1e_s"], 1)

            def w1_lo(e, j):
                c, half = j // 2, slice((j % 2) * (FF // 2), (j % 2 + 1) * (FF // 2))
                dve.wait_ge(s["w1_hi_s"], DC * e + c + 1)
                dve.scalar_tensor_tensor(w1[1][:, c, half], w1r[:, c, half], FS, w1[0][:, c, half],
                                         ALU.mult, ALU.subtract).then_inc(s["w1_lo_s"], 1)

            def w2_split(e, j, first):
                rows = slice(j * (FC // 4), (j + 1) * (FC // 4))
                if j == 0:
                    dve.wait_ge(s["ld_w2"], 16 * (e + 1))
                    if not first:
                        dve.wait_ge(s["y_mm"], KT * e)
                dve.tensor_scalar(w2[0][:, rows], w2r[:, rows], FS, None, ALU.mult).then_inc(s["w2_hi_s"], 1)
                dve.wait_ge(s["w2_hi_s"], 4 * e + j + 1)
                dve.scalar_tensor_tensor(w2[1][:, rows], w2r[:, rows], FS, w2[0][:, rows],
                                         ALU.mult, ALU.subtract).then_inc(s["w2_lo_s"], 1)

            def ex_lo(e, i):
                dve.wait_ge(s["ex_hi"], 4 * e + i + 1)
                span = slice((i // 2) * 512, (i // 2 + 1) * 512)
                dve.scalar_tensor_tensor(exT[1][:, i % 2, span], D_[:, i % 2, :], XS, exT[0][:, i % 2, span],
                                         ALU.mult, ALU.subtract).then_inc(s["ex_lo"], 1)

            def expert(e, first, last):
                b1_of(e, first)
                for u in range(2 * FC):
                    h, f = u // FC, u % FC
                    dve.wait_ge(s["h_hi"], 2 * FC * e + u + 1)
                    dve.tensor_tensor(hid[1][:, f, h * 512:(h + 1) * 512], g32[:, u % 2, :], hid[0][:, f, h * 512:(h + 1) * 512],
                                      ALU.subtract).then_inc(s["h_lo"], 1)
                    if u == 0 and not last:
                        places(e + 1, False)
                    if u % 2 and u // 2 < 4:
                        w2_split(e, u // 2, first)
                    if 1 <= u <= 11 and not last:
                        onehot(3 * (u - 1), min(3 * u, NT))
                    if u == 12:
                        keep(e, first)
                if not last:
                    ids_of(e + 1, False)
                for t in range(KT):
                    dve.wait_ge(s["y_mm"], KT * e + t + 1)
                    if t == 0:
                        dve.wait_ge(s["b2e_s"], e + 1)
                    if not (first and t < 2):
                        dve.wait_ge(s["y_o"], KT * e + t - 1)
                    dve.scalar_tensor_tensor(yt[:, t % 2, :], C_[:, t % 2, 0:D], 1.0 / FS, b2e[:],
                                             ALU.mult, ALU.add).then_inc(s["y_t"], 1)
                    if not last and t < 4:
                        w1_lo(e + 1, t)
                    if not last and t >= KT - 4:
                        ex_lo(e + 1, t - (KT - 4))

            places(0, True)
            onehot(0, NT)
            ids_of(0, True)
            for j in range(4):
                w1_lo(0, j)
            for i in range(4):
                ex_lo(0, i)
            dve.wait_ge(s["ld_b2"], 16 * E)
            expert(0, True, False)
            with dve.Fori(1, E - 1) as e:
                expert(e, False, False)
            expert(E - 1, False, True)

        @block.tensor
        def _(pe):
            def pairs(out, lhs, rhs, chunks):
                terms = [(a, b, c) for c in range(chunks) for a, b in ((0, 0), (0, 1), (1, 0))]
                for i, (a, b, c) in enumerate(terms):
                    last = pe.matmul(out, lhs(a, c), rhs(b, c), start=i == 0, stop=i == len(terms) - 1)
                return last

            def transposes(out, src, tiles_, chunks):
                for t in range(tiles_):
                    for c in range(chunks):
                        last = pe.transpose(out[:, c, t * P:(t + 1) * P], src[:, t, c * P:(c + 1) * P], ident[:])
                return last

            wsp = [w_hi, w_lo]
            pe.wait_ge(s["const1"], 4)
            pe.wait_ge(s["xn_rdy"], TP)
            transposes(B_, xn, TP, DC).then_inc(s["x_tr"], 1)
            pe.wait_ge(s["ld_ctx"], 16)
            transposes(C_, ctx, TP, DC).then_inc(s["c_tr"], 1)
            pe.wait_ge(s["ld_b"], 48)
            NR = NB1 + 2 * DC
            pe.transpose(D_[:, 1, 0:NR], brow[:], ident[0:NR, 0:NR]).then_inc(s["b_tr"], 1)
            pe.wait_ge(s["w_lo_s"], 1)
            pe.wait_ge(s["ld_wg"], 16)
            pe.wait_ge(s["b_col"], 1)

            def body(n, k):
                if runs(n, k, 0):
                    pe.wait_ge(s["x_lo"], n + 1)
                    if k != 0:
                        pe.wait_ge(s["v_lo"], n)
                    for e in range(DC):
                        last = pairs(A_[:, e, :], lambda a, d: wsp[a][:, 0, d, e * P:(e + 1) * P], lambda b, d: xT[b][:, d, :], DC)
                    last.then_inc(s["q_mm"], 1)
                if runs(n, k, 2):
                    pe.wait_ge(s["xn2_rdy"], TP * (n - 1))
                    pe.wait_ge(s["c_lo"], n + 1 if k is None or k < NP else NP)
                    if k != 2:
                        pe.wait_ge(s["l_ev"], n - 2)
                    transposes(C_, xn2, TP, DC).then_inc(s["x2_tr"], 1)
                if runs(n, k, 0):
                    pe.wait_ge(s["c_lo"], n + 1)
                    for e in range(DC):
                        last = pairs(D_[:, e, :], lambda a, d: wsp[a][:, 1, d, e * P:(e + 1) * P], lambda b, d: cT[b][:, d, :], DC)
                    last.then_inc(s["k_mm"], 1)
                if runs(n, k, 1):
                    pe.wait_ge(s["s_exp"], TP * n)
                    transposes(B_, prob, TP, SC).then_inc(s["p_tr"], 1)
                if runs(n, k, 2):
                    pe.wait_ge(s["x2_ev"], n - 1)
                    for t in range(TP):
                        for d in range(DC):
                            last = pe.matmul(C_[:, 0, t * E:(t + 1) * E], xn2T[:, d, t * P:(t + 1) * P], wg[:, d, :],
                                             start=d == 0, stop=d == DC - 1)
                    last.then_inc(s["l_mm"], 1)
                if runs(n, k, 0):
                    pe.wait_ge(s["q_lo"], DC * (n + 1))
                    for t in range(TP):
                        last = pairs(A_[:, t // 2, (t % 2) * D:(t % 2 + 1) * D], lambda a, d: cT[a][:, d, t * P:(t + 1) * P],
                                     lambda b, d: wsp[b][:, 2, d, :], DC)
                    last.then_inc(s["v_mm"], 1)
                if runs(n, k, 1):
                    pe.wait_ge(s["p_lo"], n)
                    pe.wait_ge(s["v_lo"], n)
                    for t in range(TP):
                        last = pairs(B_[:, t // 2, (t % 2) * D:(t % 2 + 1) * D], lambda a, c: pT[a][:, c, t * P:(t + 1) * P],
                                     lambda b, c: v[b][:, (t // SC) * SC + c, :], SC)
                    last.then_inc(s["o_mm"], 1)
                if runs(n, k, -1):
                    pe.wait_ge(s["xn_rdy"], TP * (n + 2))
                    pe.wait_ge(s["k_lo"], DC * (n + 1))
                    transposes(D_, xn, TP, DC).then_inc(s["x_tr"], 1)
                    pe.wait_ge(s["ld_ctx"], 16 * (n + 2))
                    if k is None or k >= 2:
                        pe.wait_ge(s["l_ev"], n - 1)
                    transposes(C_, ctx, TP, DC).then_inc(s["c_tr"], 1)
                if runs(n, k, 0):
                    pe.wait_ge(s["q_lo"], DC * (n + 1))
                    pe.wait_ge(s["k_lo"], DC * (n + 1))
                    if k != 0:
                        pe.wait_ge(s["o_ev"], TP * n)
                    for t in range(TP):
                        b0 = (t // SC) * S
                        last = pairs(B_[:, t // 2, (t % 2) * S:(t % 2 + 1) * S], lambda a, e: qT[a][:, e, t * P:(t + 1) * P],
                                     lambda b, e: kT[b][:, e, b0:b0 + S], DC)
                    last.then_inc(s["s_mm"], 1)

            phase_a(pe, body)

            pe.wait_ge(s["gate_r"], 1)
            for h in range(2):
                last = pe.transpose(A_[:, 0, h * P:(h + 1) * P], gate[:, h * HT:(h + 1) * HT, :].rearrange("p t e -> p (t e)"), ident[:])
            last.then_inc(s["key_tr"], 1)
            pe.wait_ge(s["same_s"], 1)
            with pe.Fori(0, ROUNDS) as r:
                pe.wait_ge(s["srch_cmp"], 3 * (r + 1))
                pe.matmul(A_[:, 1, 0:3], same16[:], cnt[:], start=True, stop=True).then_inc(s["srch_mm"], 1)
            pe.wait_ge(s["kq_s"], 1)
            pe.wait_ge(s["key_ev"], 1)
            pe.matmul(A_[:, 0, 0:E], onesf[:], kth_q[:], start=True, stop=True).then_inc(s["kq_mm"], 1)
            pe.wait_ge(s["above_s"], 2)
            flags = above[:].rearrange("p a t e -> p (a t e)")
            pe.matmul(C_[:, 0, :], ones16[:], flags, start=True, stop=True).then_inc(s["tot_mm"], 1)
            pe.matmul(B_[:, 0, :], before16[:], flags, start=True, stop=True).then_inc(s["pref_mm"], 1)

            def list_of(e, first):
                pe.wait_ge(s["val_s"], 2 * (e + 1))
                for t in range(NT):
                    if t % 8 == 0:
                        pe.wait_ge(s["hot_s"], NT * e + t + 8)
                    last = pe.matmul(D_[:, 0, 0:2 * KT], oneh[:, t, :], val[:, t].rearrange("p a j -> p (a j)"),
                                     start=t == 0, stop=t == NT - 1)
                last.then_inc(s["id_mm"], 1)

            def rows_T(e, i, first):
                if i == 0:
                    pe.wait_ge(s["gat"], 16 * KT * (e + 1))
                    pe.wait_ge(s["id_ev"], e + 1)
                if i >= 2:
                    pe.wait_ge(s["ex_lo"], 4 * e + i - 1)
                for j in range(4):
                    last = pe.transpose(D_[:, i % 2, j * P:(j + 1) * P], ex[:, (i // 2) * 4 + j, (i % 2) * P:(i % 2 + 1) * P], ident[:])
                last.then_inc(s["ex_tr"], 1)

            def expert(e, first, last_one):
                pe.wait_ge(s["ex_lo"], 4 * (e + 1))
                pe.wait_ge(s["w1_lo_s"], 4 * (e + 1))
                for u in range(2 * FC):
                    h, f = u // FC, u % FC
                    if not (first and u < 4):
                        pe.wait_ge(s["h_hi"], 2 * FC * e + u - 3)
                    pairs(bank[(u % 4) // 2][:, u % 2, :], lambda a, c: w1[a][:, c, f * P:(f + 1) * P],
                          lambda b, c: exT[b][:, c, h * 512:(h + 1) * 512], DC).then_inc(s["h_mm"], 1)
                if not last_one:
                    list_of(e + 1, False)
                pe.wait_ge(s["w2_lo_s"], 4 * (e + 1))
                for t in range(KT):
                    if t % (KT // 2) == 0:
                        pe.wait_ge(s["h_lo"], 2 * FC * e + FC * (t // (KT // 2) + 1))
                    if not (first and t < 2):
                        pe.wait_ge(s["y_t"], KT * e + t - 1)
                    pairs(C_[:, t % 2, 0:D], lambda a, f: hid[a][:, f, t * P:(t + 1) * P],
                          lambda b, f: w2[b][:, f, :], FC).then_inc(s["y_mm"], 1)
                    if not last_one and t >= KT - 5 and t < KT - 1:
                        rows_T(e + 1, t - (KT - 5), False)

            pe.wait_ge(s["l_ev"], NP)
            list_of(0, True)
            for i in range(4):
                rows_T(0, i, True)
            expert(0, True, False)
            with pe.Fori(1, E - 1) as e:
                expert(e, False, False)
            expert(E - 1, False, True)


INS = ["x", "ctx_1024", "L0_xattn_Wq", "L0_xattn_bq", "L0_xattn_Wk", "L0_xattn_bk", "L0_xattn_Wv", "L0_xattn_bv",
       "L0_ffn_Wg", "L0_ffn_W1", "L0_ffn_b1", "L0_ffn_W2", "L0_ffn_b2"]


def kernel(**inputs):
    import concourse.bacc as bacc
    from concourse.bass_utils import run_bass_kernel_spmd

    nc = bacc.Bacc("TRN2", target_bir_lowering=False, num_devices=1)
    arrays, args = {}, []
    for name in INS:
        a = np.ascontiguousarray(inputs[name])
        arrays[f"in_{name}"] = a
        args.append(nc.dram_tensor(f"in_{name}", a.shape, mybir.dt.from_np(a.dtype), kind="ExternalInput").ap())
    out = nc.dram_tensor("out", inputs["x"].shape, F32, kind="ExternalOutput").ap()
    build(nc, *args, out)
    r = run_bass_kernel_spmd(nc, [arrays], core_ids=[0])
    return r.results[0]["out"]
```

```python
import math
from contextlib import ExitStack

import numpy as np
import concourse.bass as bass
from concourse import mybir

F32 = mybir.dt.float32
F16 = mybir.dt.float16
BF16 = mybir.dt.bfloat16
I32 = mybir.dt.int32
ALU = mybir.AluOpType
ACT = mybir.ActivationFunctionType
AX = mybir.AxisListType

P = 128


def build(nc, x_d, ctx_d, wq_d, bq_d, wk_d, bk_d, wv_d, bv_d, wg_d, w1_d, b1_d, w2_d, b2_d, out_d):
    B, S, D = x_d.shape
    E, _, FF = w1_d.shape
    N = B * S
    K = max(N * 2 // E, 1)
    NT = N // P
    TP = 4
    NP = NT // TP
    PT_ = TP * P
    DC = D // P
    FC = FF // P
    KT = K // P
    SC = S // P
    EPS = 1e-5

    XS = 4.0
    AS = 16.0
    QS = XS * AS
    PS = 4096.0
    FS = 256.0
    SCORE = 1.0 / (QS * QS * math.sqrt(D))
    BITS = 30
    ROUNDS = BITS // 2
    KEEP = 5
    SPLIT = 2
    NOWHERE = float(N)

    with ExitStack() as stack:
        def sb(name, shape, dt=F32):
            return stack.enter_context(nc.sbuf_tensor(name, shape, dt))

        def sem(name):
            return stack.enter_context(nc.semaphore(name))

        rows_d = nc.dram_tensor("rows_d", [N, D + E], F32).ap()

        ident = sb("ident", [P, P])
        ones16 = sb("ones16", [P, P], BF16)
        before16 = sb("before16", [P, P], BF16)
        same16 = sb("same16", [P, P], BF16)
        apart = sb("apart", [P, P], I32)
        onesf = sb("onesf", [P, P])
        pick = sb("pick", [P, E])
        iota16 = sb("iota16", [P, P], BF16)
        iota8 = sb("iota8", [P, NT, KT])
        tileno = sb("tileno", [P, NT, KT])
        partno = sb("partno", [P, 1])
        mhalf = sb("mhalf", [P, TP])
        eps = sb("eps", [P, TP]); minus = sb("minus", [P, TP])
        dve_tick = sb("dve_tick", [P, 1]); pool_tick = sb("pool_tick", [P, KT + 1])
        w_raw = sb("w_raw", [P, 3, DC, D])
        w_hi = sb("w_hi", [P, 3, DC, D], F16)
        w_lo = sb("w_lo", [P, 3, DC, D], F16)
        wg = sb("wg", [P, DC, E])
        NB1 = E * FC
        brow = sb("brow", [NB1 + 2 * DC, P])
        bcol = sb("bcol", [P, NB1 + 2 * DC])
        bqk = sb("bqk", [P, 2 * DC])
        bv_bc = sb("bv_bc", [P, TP, D])
        b2_bc = sb("b2_bc", [P, E, D])
        xres = sb("xres", [P, NT, D])
        ctx = sb("ctx", [P, TP, D])
        xn = sb("xn", [P, TP, D])
        xn2 = sb("xn2", [P, TP, D])
        st1 = sb("st1", [P, TP, 6]); mv1 = sb("mv1", [P, TP, 2])
        rstd1 = sb("rstd1", [P, TP]); nmr1 = sb("nmr1", [P, TP])
        st2 = sb("st2", [P, TP, 6]); mv2 = sb("mv2", [P, TP, 2])
        rstd2 = sb("rstd2", [P, TP]); nmr2 = sb("nmr2", [P, TP])
        xT = [sb(f"xT{i}", [P, DC, PT_], F16) for i in "hl"]
        cT = [sb(f"cT{i}", [P, DC, PT_], F16) for i in "hl"]
        qT = [sb(f"qT{i}", [P, DC, PT_], F16) for i in "hl"]
        kT = [sb(f"kT{i}", [P, DC, PT_], F16) for i in "hl"]
        v = [sb(f"v{i}", [P, TP, D], F16) for i in "hl"]
        prob = sb("prob", [P, TP, S])
        pT = [sb(f"pT{i}", [P, SC, PT_], F16) for i in "hl"]
        nmax = sb("nmax", [P, TP]); nbias = sb("nbias", [P, TP])
        rsum = sb("rsum", [P, TP]); rinv = sb("rinv", [P, TP]); rinvs = sb("rinvs", [P, TP])
        xn2T = sb("xn2T", [P, DC, PT_])
        logit = sb("logit", [P, NT, E])
        gate = sb("gate", [P, NT, E])
        HT = NT // 2
        keyT = sb("keyT", [P, 2, P])
        junk = sb("junk", [P, 3, 2, P], BF16)
        steps = sb("steps", [P, 3], I32)
        found = sb("found", [P, 3], I32)
        gain = sb("gain", [P, 1], I32)
        base = sb("base", [P, 1], I32)
        trial = sb("trial", [P, 3], I32)
        cnt = sb("cnt", [P, 3], BF16)
        kth_q = sb("kth_q", [P, E])
        kth = sb("kth", [P, E])
        above = sb("above", [P, 2, NT, E], BF16)
        run = [sb(f"run{i}", [P, 2, NT + 1, E]) for i in range(2)]
        place = sb("place", [P, 2, NT, E])
        pos = sb("pos", [P, NT, E], I32)
        loi = sb("loi", [P, NT, E], I32); hii = sb("hii", [P, NT, E], I32)
        lof = sb("lof", [P, NT, E]); hif = sb("hif", [P, NT, E])
        lo_e = sb("lo_e", [P, NT])
        oneh = sb("oneh", [P, NT, P], BF16)
        inhi = sb("inhi", [P, NT, KT])
        val = sb("val", [P, NT, 2, KT], BF16)
        idp = sb("idp", [P, 2, KT])
        ids = sb("ids", [P, KT], I32)
        ids_s = sb("ids_s", [P, KT], I32)
        ex = sb("ex", [P, KT, D + E])
        ge = sb("ge", [P, KT])
        exT = [sb(f"exT{i}", [P, DC, K], F16) for i in "hl"]
        w1r = sb("w1r", [P, DC, FF]); w2r = sb("w2r", [P, FC, D])
        w1 = [sb(f"w1{i}", [P, DC, FF], F16) for i in "hl"]
        w2 = [sb(f"w2{i}", [P, FC, D], F16) for i in "hl"]
        b1e = sb("b1e", [P, FC])
        b2e = sb("b2e", [P, D])
        g32 = sb("g32", [P, 2, PT_])
        hid = [xres[:, i * NT // 2:(i + 1) * NT // 2, :].bitcast(F16).rearrange("p t d -> p (t d)")
               .rearrange("p (f k) -> p f k", f=FC) for i in range(2)]
        yt = sb("yt", [P, 2, D])
        yo = sb("yo", [P, KT, D])

        bank = [stack.enter_context(nc.psum_tensor(f"bank{i}", [P, 2, 512], F32)) for i in range(4)]
        A_, B_, C_, D_ = bank

        names = """ld_x0 ld_x1 ld_w ld_wg ld_b ld_bv ld_b2 ld_ctx const0 const1 const2 and_s same_s
            w_hi_s w_lo_s b_tr b_col b_qk
            ln1_st ln1_mv ln1_eps ln1_rstd ln1_mr ln1_nmr xn_rdy xbv
            x_tr x_hi x_lo c_tr c_hi c_lo q_mm q_hi q_lo k_mm k_hi k_lo v_mm v_hi v_lo
            s_mm s_max s_nb s_exp s_ri s_ris p_tr p_hi p_lo o_mm o_ev
            ln2_st ln2_mv ln2_eps ln2_rstd ln2_mr ln2_nmr xn2_rdy st_x1 st_xn
            x2_tr x2_ev l_mm l_ev
            gate_r st_gate key_tr key_ev init_s srch_tr srch_cmp srch_mm srch_sel srch_red srch_base srch_step
            kq_s kq_mm kth_s above_s pref_mm tot_mm run_s place_s pos_a pos_s split_i split_f
            lo_s hot_s hi_s val_s id_mm id_ev ids_s_ idss_s gat_a gat_b ge_s ex_tr ex_hi ex_lo
            ld_w1 ld_w2 w1_hi_s w1_lo_s w2_hi_s w2_lo_s b1e_s b2e_s
            h_mm h_g h_hi h_lo y_mm y_t y_o sc_done tick_g tick_s""".split()
        s = {n: sem(n) for n in names}

        block = stack.enter_context(nc.Block())
        MID0, MID1 = 3, NP - 3

        def phase_a(engine, body):
            for n in range(MID0):
                body(n, n)
            with engine.Fori(MID0, MID1 + 1) as n:
                body(n, None)
            for n in range(MID1 + 1, NP + 2):
                body(n, n)

        def runs(n, k, shift):
            return k is None or 0 <= k - shift < NP

        def tiles(n):
            return bass.ds(n * TP, TP)

        @block.sync
        def _(sp):
            xv = x_d.rearrange("b (c p) d -> p (b c) d", p=P)
            cv = ctx_d.rearrange("b (c p) d -> p (b c) d", p=P)
            ov = out_d.rearrange("b (c p) d -> p (b c) d", p=P)
            rv = rows_d.rearrange("(t p) d -> p t d", p=P)
            sp.dma_start(xres[:, 0:TP, :], xv[:, 0:TP, :]).then_inc(s["ld_x0"], 16)
            sp.dma_start(ctx[:, :, :], cv[:, 0:TP, :]).then_inc(s["ld_ctx"], 16)
            for i, w_d in enumerate((wq_d, wk_d, wv_d)):
                sp.dma_start(w_raw[:, i], w_d.rearrange("(c p) e -> p c e", p=P)).then_inc(s["ld_w"], 16)
            sp.dma_start(brow[0:NB1, :], b1_d.rearrange("e (f p) -> (e f) p", p=P)).then_inc(s["ld_b"], 16)
            sp.dma_start(brow[NB1:NB1 + DC, :], bq_d.rearrange("(f p) -> f p", p=P)).then_inc(s["ld_b"], 16)
            sp.dma_start(brow[NB1 + DC:NB1 + 2 * DC, :], bk_d.rearrange("(f p) -> f p", p=P)).then_inc(s["ld_b"], 16)
            sp.dma_start(xres[:, TP:NT, :], xv[:, TP:NT, :]).then_inc(s["ld_x1"], 16)
            sp.dma_start(wg[:, :, :], wg_d.rearrange("(c p) e -> p c e", p=P)).then_inc(s["ld_wg"], 16)
            for t in range(TP):
                sp.dma_start(bv_bc[:, t, :], bv_d.partition_broadcast(P)).then_inc(s["ld_bv"], 16)
            for e in range(E):
                sp.dma_start(b2_bc[:, e, :], b2_d[e, :].partition_broadcast(P)).then_inc(s["ld_b2"], 16)
            sp.dma_start(w1r[:, :, :], w1_d[0].rearrange("(c p) f -> p c f", p=P)).then_inc(s["ld_w1"], 16)
            sp.dma_start(w2r[:, :, :], w2_d[0].rearrange("(c p) f -> p c f", p=P)).then_inc(s["ld_w2"], 16)

            def body(n, k):
                if runs(n, k, -1):
                    sp.wait_ge(s["c_tr"], n + 1)
                    sp.dma_start(ctx[:, :, :], cv[:, tiles(n + 1), :]).then_inc(s["ld_ctx"], 16)
                if runs(n, k, 1):
                    sp.wait_ge(s["o_ev"], TP * n)
                    sp.dma_start(ov[:, tiles(n - 1), :], xres[:, tiles(n - 1), :]).then_inc(s["st_x1"], 16)
                    sp.wait_ge(s["xn2_rdy"], TP * n)
                    sp.dma_start(rv[:, tiles(n - 1), 0:D], xn2[:, :, :]).then_inc(s["st_xn"], 16)

            phase_a(sp, body)
            sp.wait_ge(s["gate_r"], 1)
            sp.dma_start(rv[:, :, D:D + E], gate[:, :, :]).then_inc(s["st_gate"], 16)
            with sp.Fori(1, E) as e:
                sp.wait_ge(s["w1_lo_s"], 4 * e)
                sp.dma_start(w1r[:, :, :], w1_d[bass.ds(e, 1)].rearrange("o (c p) f -> p (o c) f", p=P)).then_inc(s["ld_w1"], 16)
                sp.wait_ge(s["w2_lo_s"], 4 * e)
                sp.dma_start(w2r[:, :, :], w2_d[bass.ds(e, 1)].rearrange("o (c p) f -> p (o c) f", p=P)).then_inc(s["ld_w2"], 16)
            sp.wait_ge(s["sc_done"], 16 * KT * E)
            sp.wait_ge(s["st_x1"], 16 * NP)
            sp.wait_ge(s["st_xn"], 16 * NP)
            sp.wait_ge(s["st_gate"], 16)

        @block.gpsimd
        def _(pool):
            pool.memset(ident[:], 0.0).then_inc(s["const0"], 1)
            pool.memset(before16[:], 1.0).then_inc(s["const0"], 1)
            pool.memset(pick[:], 0.0).then_inc(s["const0"], 1)
            pool.wait_ge(s["const0"], 3)
            pool.affine_select(out=ident[:], in_=ident[:], compare_op=ALU.not_equal, fill=1.0, base=0,
                               pattern=[[-1, P]], channel_multiplier=1).then_inc(s["const1"], 1)
            pool.affine_select(out=before16[:], in_=before16[:], compare_op=ALU.is_gt, fill=0.0, base=0,
                               pattern=[[1, P]], channel_multiplier=-1).then_inc(s["const1"], 1)
            pool.affine_select(out=pick[:], in_=pick[:], compare_op=ALU.not_equal, fill=1.0, base=0,
                               pattern=[[-1, E]], channel_multiplier=1).then_inc(s["const1"], 1)
            pool.memset(mhalf[:], -0.5).then_inc(s["const1"], 1)
            pool.memset(eps[:], EPS).then_inc(s["const1"], 1)
            pool.memset(minus[:], -1.0).then_inc(s["const1"], 1)
            pool.memset(ones16[:], 1.0).then_inc(s["const1"], 1)
            pool.memset(onesf[:], 1.0).then_inc(s["const1"], 1)

            def ln_scale(mv, rstd, nmr, a, n):
                pool.tensor_tensor(rstd[:], mv[:, :, 1], eps[:], ALU.add).then_inc(s[a + "_eps"], 1)
                pool.wait_ge(s[a + "_eps"], n + 1)
                pool.tensor_tensor(rstd[:], rstd[:], mhalf[:], ALU.pow).then_inc(s[a + "_rstd"], 1)
                pool.wait_ge(s[a + "_rstd"], n + 1)
                pool.tensor_tensor(nmr[:], mv[:, :, 0], rstd[:], ALU.mult).then_inc(s[a + "_mr"], 1)
                pool.wait_ge(s[a + "_mr"], n + 1)
                pool.tensor_tensor(nmr[:], nmr[:], minus[:], ALU.mult).then_inc(s[a + "_nmr"], 1)

            def ln1(n, first=False):
                pool.wait_ge(s["ln1_mv"], TP * (n + 1))
                if not first:
                    pool.wait_ge(s["xn_rdy"], TP * n)
                ln_scale(mv1, rstd1, nmr1, "ln1", n)

            def add_bv(n):
                pool.wait_ge(s["xn_rdy"], TP * (n + 1))
                pool.tensor_tensor(xres[:, tiles(n), :], xres[:, tiles(n), :], bv_bc[:], ALU.add).then_inc(s["xbv"], 1)

            pool.wait_ge(s["const1"], 6)
            ln1(0, True)
            pool.iota(apart[:], [[1, P]], base=P, channel_multiplier=-1).then_inc(s["const2"], 1)
            pool.iota(iota16[:], [[1, P]], base=0, channel_multiplier=0, allow_small_or_imprecise_dtypes=True).then_inc(s["const2"], 1)
            pool.iota(iota8[:], [[0, NT], [1, KT]], base=0, channel_multiplier=0, allow_small_or_imprecise_dtypes=True).then_inc(s["const2"], 1)
            pool.iota(tileno[:], [[1, NT], [0, KT]], base=0, channel_multiplier=0, allow_small_or_imprecise_dtypes=True).then_inc(s["const2"], 1)
            pool.iota(partno[:], [[0, 1]], base=0, channel_multiplier=1, allow_small_or_imprecise_dtypes=True).then_inc(s["const2"], 1)
            pool.wait_ge(s["ld_bv"], 16 * TP)
            add_bv(0)

            def body(n, k):
                if runs(n, k, -1):
                    ln1(n + 1)
                    add_bv(n + 1)
                if runs(n, k, 1):
                    pool.wait_ge(s["ln2_mv"], TP * n)
                    if k != 1:
                        pool.wait_ge(s["xn2_rdy"], TP * (n - 1))
                    ln_scale(mv2, rstd2, nmr2, "ln2", n - 1)

            phase_a(pool, body)

            rows_out = out_d.rearrange("b s d -> (b s) d")

            def gather(e, first):
                pool.wait_ge(s["ids_s_"], e + 1)
                if not first:
                    pool.wait_ge(s["ex_tr"], 4 * e)
                    pool.wait_ge(s["ge_s"], e)
                    pool.wait_ge(s["tick_g"], e)
                pool.tensor_tensor(pool_tick[:, 0:1], eps[:, 0:1], eps[:, 0:1], ALU.add).then_inc(s["tick_g"], 1)
                for t in range(KT):
                    pool.indirect_dma_start(out=ex[:, t, :], out_offset=None, in_=rows_d,
                                            in_offset=bass.IndirectOffsetOnAxis(ap=ids[:, t:t + 1], axis=0)
                                            ).then_inc(s["gat_a"] if t < KT // 2 else s["gat_b"], 16)

            def scatter(e, first):
                if not first:
                    pool.wait_ge(s["sc_done"], 16 * KT * e)
                for t in range(KT):
                    pool.wait_ge(s["y_o"], KT * e + t + 1)
                    if not first:
                        pool.wait_ge(s["tick_s"], KT * (e - 1) + t + 1)
                    pool.tensor_tensor(pool_tick[:, t + 1:t + 2], eps[:, 0:1], eps[:, 0:1], ALU.add).then_inc(s["tick_s"], 1)
                    pool.indirect_dma_start(out=rows_out, out_offset=bass.IndirectOffsetOnAxis(ap=ids_s[:, t:t + 1], axis=0),
                                            in_=yo[:, t, :], in_offset=None, compute_op=ALU.add).then_inc(s["sc_done"], 16)

            pool.wait_ge(s["st_xn"], 16 * NP)
            pool.wait_ge(s["st_gate"], 16)
            gather(0, True)
            pool.wait_ge(s["st_x1"], 16 * NP)
            gather(1, False)
            scatter(0, True)
            with pool.Fori(1, E - 1) as e:
                gather(e + 1, False)
                scatter(e, False)
            scatter(E - 1, False)

        @block.scalar
        def _(act):
            def hi(dst, src, mm, done, count, scale=1.0, bias=0.0, func=ACT.Identity):
                act.wait_ge(s[mm], count)
                act.activation(dst, src, func, bias=bias, scale=scale).then_inc(s[done], 1)

            def apply_ln(dst, rstd, nmr, a, n, done):
                act.wait_ge(s[a + "_nmr"], n + 1)
                for t in range(TP):
                    act.activation(dst[:, t, :], xres[:, bass.ds(n * TP + t, 1), :].rearrange("p o d -> p (o d)"), ACT.Identity,
                                   bias=nmr[:, t:t + 1], scale=rstd[:, t:t + 1]).then_inc(s[done], 1)

            apply_ln(xn, rstd1, nmr1, "ln1", 0, "xn_rdy")
            act.wait_ge(s["ld_w"], 48)
            act.activation(w_hi[:], w_raw[:], ACT.Copy, scale=AS).then_inc(s["w_hi_s"], 1)
            act.wait_ge(s["b_tr"], 1)
            act.activation(bcol[:], A_[:, 1, 0:NB1 + 2 * DC], ACT.Copy).then_inc(s["b_col"], 1)
            hi(xT[0][:], D_[:], "x_tr", "x_hi", 1, scale=XS)
            hi(cT[0][:], C_[:], "c_tr", "c_hi", 1, scale=XS)
            act.wait_ge(s["b_qk"], 1)

            def body(n, k):
                if runs(n, k, 0):
                    for c in range(DC):
                        act.wait_ge(s["q_mm"], DC * n + c + 1)
                        if k != 0 and c == 0:
                            act.wait_ge(s["s_mm"], n)
                        act.activation(qT[0][:, c, :], A_[:, c, :], ACT.Identity, bias=bqk[:, c:c + 1]).then_inc(s["q_hi"], 1)
                    for c in range(DC):
                        act.wait_ge(s["k_mm"], DC * n + c + 1)
                        act.activation(kT[0][:, c, :], D_[:, c, :], ACT.Identity, bias=bqk[:, DC + c:DC + c + 1]).then_inc(s["k_hi"], 1)
                if runs(n, k, 2):
                    act.wait_ge(s["x2_tr"], n - 1)
                    if k != 2:
                        act.wait_ge(s["l_mm"], n - 2)
                    act.activation(xn2T[:], C_[:], ACT.Copy).then_inc(s["x2_ev"], 1)
                if runs(n, k, 1):
                    if k != 1:
                        act.wait_ge(s["o_mm"], TP * (n - 1))
                    hi(pT[0][:], B_[:], "p_tr", "p_hi", n)
                if runs(n, k, -1):
                    act.wait_ge(s["x_tr"], n + 1)
                    apply_ln(xn, rstd1, nmr1, "ln1", n + 1, "xn_rdy")
                if runs(n, k, 0):
                    act.wait_ge(s["v_mm"], n + 1)
                    if k != 0:
                        act.wait_ge(s["o_mm"], TP * n)
                    act.activation(v[0][:], A_[:].rearrange("p a (b d) -> p (a b) d", d=D), ACT.Identity).then_inc(s["v_hi"], 1)
                if runs(n, k, -1):
                    hi(xT[0][:], D_[:], "x_tr", "x_hi", n + 2, scale=XS)
                    hi(cT[0][:], C_[:], "c_tr", "c_hi", n + 2, scale=XS)
                if runs(n, k, 1):
                    if k != 1:
                        act.wait_ge(s["x2_tr"], n - 1)
                        act.wait_ge(s["st_xn"], 16 * (n - 1))
                    apply_ln(xn2, rstd2, nmr2, "ln2", n - 1, "xn2_rdy")
                if runs(n, k, 0):
                    act.wait_ge(s["s_nb"], n + 1)
                    if k != 0:
                        act.wait_ge(s["p_tr"], n)
                        act.wait_ge(s["s_ri"], n)
                    for t in range(TP):
                        act.activation(prob[:, t, :], B_[:, t // 2, (t % 2) * S:(t % 2 + 1) * S], ACT.Exp,
                                       bias=nbias[:, t:t + 1], scale=SCORE,
                                       accum_out=rsum[:, t:t + 1]).then_inc(s["s_exp"], 1)

            phase_a(act, body)
            act.wait_ge(s["l_ev"], NP)
            act.activation(gate[:], logit[:], ACT.Sigmoid).then_inc(s["gate_r"], 1)
            act.wait_ge(s["key_tr"], 1)
            act.activation(keyT[:], A_[:, 0, 0:2 * P].rearrange("p (a b) -> p a b", a=2), ACT.Copy).then_inc(s["key_ev"], 1)

            def w1_hi(e, c):
                act.activation(w1[0][:, c], w1r[:, c], ACT.Copy, scale=FS).then_inc(s["w1_hi_s"], 1)

            def ex_hi(e, i):
                act.wait_ge(s["ex_tr"], 4 * e + i + 1)
                act.activation(exT[0][:, i % 2, (i // 2) * 512:(i // 2 + 1) * 512], D_[:, i % 2, :],
                               ACT.Copy, scale=XS).then_inc(s["ex_hi"], 1)

            def layer1(e, first):
                act.wait_ge(s["b1e_s"], e + 1)
                for u in range(2 * FC):
                    h, f = u // FC, u % FC
                    if first and u == SPLIT:
                        ex_hi(0, 2)
                        ex_hi(0, 3)
                    act.wait_ge(s["h_mm"], 2 * FC * e + u + 1)
                    src = bank[(u % 4) // 2][:, u % 2, :]
                    if not (first and u < 2):
                        act.wait_ge(s["h_lo"], 2 * FC * e + u - 1)
                    act.activation(g32[:, u % 2, :], src, ACT.Gelu, bias=b1e[:, f:f + 1],
                                   scale=1.0 / (XS * FS)).then_inc(s["h_g"], 1)
                    if not first and f == 0:
                        act.wait_ge(s["y_mm"], KT * (e - 1) + (KT // 2) * (h + 1))
                    act.activation(hid[0][:, f, h * 512:(h + 1) * 512], src, ACT.Gelu, bias=b1e[:, f:f + 1],
                                   scale=1.0 / (XS * FS)).then_inc(s["h_hi"], 1)

            def layer2(e, first, last):
                act.wait_ge(s["ge_s"], e + 1)
                if not first:
                    act.wait_ge(s["sc_done"], 16 * KT * e)
                if not last:
                    act.wait_ge(s["ld_w1"], 16 * (e + 2))
                for t in range(KT):
                    if not last and t < DC:
                        w1_hi(e + 1, t)
                    act.wait_ge(s["y_t"], KT * e + t + 1)
                    act.activation(yo[:, t, :], yt[:, t % 2, :], ACT.Copy, scale=ge[:, t:t + 1]).then_inc(s["y_o"], 1)
                    if not last and t < 4:
                        ex_hi(e + 1, t)

            act.wait_ge(s["ld_w1"], 16)
            for c in range(DC):
                w1_hi(0, c)
            for i in range(2):
                ex_hi(0, i)
            act.wait_ge(s["st_x1"], 16 * NP)
            layer1(0, True)
            layer2(0, True, False)
            with act.Fori(1, E - 1) as e:
                layer1(e, False)
                layer2(e, False, False)
            layer1(E - 1, False)
            layer2(E - 1, False, True)

        @block.vector
        def _(dve):
            def stats(n, st, mv, a, src_ready, need):
                if src_ready is not None:
                    dve.wait_ge(s[src_ready], need)
                dve.memset(dve_tick[:], 0.0)
                for t in range(TP):
                    dve.bn_stats(st[:, t, :], xres[:, bass.ds(n * TP + t, 1), :].rearrange("p o d -> p (o d)")).then_inc(s[a + "_st"], 1)
                dve.wait_ge(s[a + "_st"], TP * (n + 1))
                dve.memset(dve_tick[:], 0.0)
                for t in range(TP):
                    dve.bn_aggr(mv[:, t, :], st[:, t, :]).then_inc(s[a + "_mv"], 1)

            def lo(dst, src, hi_, ready, count, done, scale=None):
                dve.wait_ge(s[ready], count)
                if scale is None:
                    dve.tensor_tensor(dst, src, hi_, ALU.subtract).then_inc(s[done], 1)
                else:
                    dve.scalar_tensor_tensor(dst, src, scale, hi_, ALU.mult, ALU.subtract).then_inc(s[done], 1)

            dve.wait_ge(s["ld_x0"], 16)
            stats(0, st1, mv1, "ln1", None, 0)
            lo(w_lo[:].rearrange("p a b c -> p (a b c)"), w_raw[:].rearrange("p a b c -> p (a b c)"), w_hi[:].rearrange("p a b c -> p (a b c)"), "w_hi_s", 1, "w_lo_s", AS)
            dve.wait_ge(s["b_col"], 1)
            dve.tensor_scalar(bqk[:], bcol[:, NB1:], QS, None, ALU.mult).then_inc(s["b_qk"], 1)
            dve.wait_ge(s["b_qk"], 1)
            lo(xT[1][:], D_[:], xT[0][:], "x_hi", 1, "x_lo", XS)
            dve.wait_ge(s["ld_x1"], 16)

            def body(n, k):
                if runs(n, k, 0):
                    lo(cT[1][:], C_[:], cT[0][:], "c_hi", n + 1, "c_lo", XS)
                if runs(n, k, -1):
                    dve.wait_ge(s["ln1_nmr"], n + 1)
                    stats(n + 1, st1, mv1, "ln1", None, 0)
                if runs(n, k, 0):
                    for c in range(DC):
                        dve.wait_ge(s["q_hi"], DC * n + c + 1)
                        dve.scalar_tensor_tensor(qT[1][:, c, :], A_[:, c, :], bqk[:, c:c + 1], qT[0][:, c, :], ALU.add, ALU.subtract).then_inc(s["q_lo"], 1)
                if runs(n, k, 1):
                    dve.wait_ge(s["s_exp"], TP * n)
                    dve.reciprocal(rinv[:], rsum[:]).then_inc(s["s_ri"], 1)
                    dve.wait_ge(s["s_ri"], n)
                    dve.tensor_scalar(rinvs[:], rinv[:], 1.0 / QS, None, ALU.mult).then_inc(s["s_ris"], 1)
                if runs(n, k, 0):
                    for c in range(DC):
                        dve.wait_ge(s["k_hi"], DC * n + c + 1)
                        dve.scalar_tensor_tensor(kT[1][:, c, :], D_[:, c, :], bqk[:, DC + c:DC + c + 1], kT[0][:, c, :], ALU.add, ALU.subtract).then_inc(s["k_lo"], 1)
                if runs(n, k, 1):
                    lo(pT[1][:], B_[:], pT[0][:], "p_hi", n, "p_lo")
                if runs(n, k, 2):
                    dve.wait_ge(s["l_mm"], n - 1)
                    dve.tensor_copy(logit[:, tiles(n - 2), :], C_[:, 0, 0:TP * E].rearrange("p (t e) -> p t e", e=E)).then_inc(s["l_ev"], 1)
                if runs(n, k, 1):
                    dve.wait_ge(s["xbv"], n)
                    dve.wait_ge(s["s_ris"], n)
                    for t in range(TP):
                        if t % 2 == 0:
                            dve.wait_ge(s["o_mm"], TP * (n - 1) + t + 2)
                        xt = xres[:, bass.ds((n - 1) * TP + t, 1), :].rearrange("p o d -> p (o d)")
                        dve.scalar_tensor_tensor(xt, B_[:, t // 2, (t % 2) * D:(t % 2 + 1) * D], rinvs[:, t:t + 1], xt,
                                                 ALU.mult, ALU.add).then_inc(s["o_ev"], 1)
                    if k != 1:
                        dve.wait_ge(s["ln2_nmr"], n - 1)
                    stats(n - 1, st2, mv2, "ln2", "o_ev", TP * n)
                if runs(n, k, 0):
                    lo(v[1][:], A_[:].rearrange("p a (b d) -> p (a b) d", d=D), v[0][:], "v_hi", n + 1, "v_lo")
                if runs(n, k, -1):
                    lo(xT[1][:], D_[:], xT[0][:], "x_hi", n + 2, "x_lo", XS)
                if runs(n, k, 0):
                    dve.wait_ge(s["s_mm"], n + 1)
                    dve.tensor_reduce(nmax[:], B_[:].rearrange("p a (b k) -> p (a b) k", k=S), AX.X, ALU.max, negate=True).then_inc(s["s_max"], 1)
                    if k != 0:
                        dve.wait_ge(s["s_exp"], TP * n)
                    dve.wait_ge(s["s_max"], n + 1)
                    dve.tensor_scalar(nbias[:], nmax[:], SCORE, math.log(PS), ALU.mult, ALU.add).then_inc(s["s_nb"], 1)

            phase_a(dve, body)

            dve.wait_ge(s["const2"], 5)
            dve.tensor_scalar(apart[:], apart[:], E - 1, None, ALU.bitwise_and).then_inc(s["and_s"], 1)
            dve.wait_ge(s["and_s"], 1)
            dve.tensor_scalar(same16[:], apart[:], 0.0, None, ALU.is_equal).then_inc(s["same_s"], 1)
            for c in range(3):
                dve.memset(steps[:, c:c + 1], (c + 1) << (BITS - 2)).then_inc(s["init_s"], 1)
            dve.memset(base[:], 0).then_inc(s["init_s"], 1)
            dve.wait_ge(s["init_s"], 4)
            dve.wait_ge(s["key_ev"], 1)
            with dve.Fori(0, ROUNDS) as r:
                dve.tensor_tensor(trial[:], steps[:], base[:, 0:1].broadcast_to([P, 3]), ALU.bitwise_or).then_inc(s["srch_tr"], 1)
                dve.wait_ge(s["srch_tr"], r + 1)
                for c in range(3):
                    dve.tensor_scalar(junk[:, c], keyT[:], trial[:, c:c + 1].bitcast(F32), None, ALU.is_ge, ALU.add,
                                      accum_out=cnt[:, c:c + 1]).then_inc(s["srch_cmp"], 1)
                dve.wait_ge(s["srch_mm"], r + 1)
                dve.scalar_tensor_tensor(found[:], A_[:, 1, 0:3], float(K), steps[:, 0:1].broadcast_to([P, 3]), ALU.is_ge, ALU.mult).then_inc(s["srch_sel"], 1)
                dve.wait_ge(s["srch_sel"], r + 1)
                with nc.allow_low_precision(reason="a sum of one to three equal powers of two"):
                    dve.tensor_reduce(gain[:], found[:], AX.X, ALU.add).then_inc(s["srch_red"], 1)
                dve.tensor_scalar(steps[:], steps[:], 2, None, ALU.logical_shift_right).then_inc(s["srch_step"], 1)
                dve.wait_ge(s["srch_red"], r + 1)
                dve.tensor_tensor(base[:], base[:], gain[:], ALU.bitwise_or).then_inc(s["srch_base"], 1)
                dve.wait_ge(s["srch_step"], r + 1)
                dve.wait_ge(s["srch_base"], r + 1)
            dve.tensor_scalar(kth_q[:], pick[:], base[:].bitcast(F32), None, ALU.mult).then_inc(s["kq_s"], 1)
            dve.wait_ge(s["kq_mm"], 1)
            dve.tensor_copy(kth[:], A_[:, 0, 0:E]).then_inc(s["kth_s"], 1)
            dve.wait_ge(s["kth_s"], 1)
            kb = kth[:, :].unsqueeze(1).broadcast_to([P, NT, E])
            dve.wait_ge(s["gate_r"], 1)
            dve.tensor_tensor(above[:, 0], gate[:], kb, ALU.is_gt).then_inc(s["above_s"], 1)
            dve.tensor_tensor(above[:, 1], gate[:], kb, ALU.is_equal).then_inc(s["above_s"], 1)
            dve.memset(run[0][:, :, 0, :], 0.0).then_inc(s["run_s"], 1)
            dve.wait_ge(s["tot_mm"], 1)
            dve.tensor_copy(run[0][:, :, 1:, :], C_[:, 0, :].rearrange("p (a t e) -> p a t e", a=2, e=E)).then_inc(s["run_s"], 1)
            dve.wait_ge(s["run_s"], 2)
            now, step, ran = 0, 1, 2
            while step <= NT:
                a, b = run[now], run[1 - now]
                dve.tensor_copy(b[:, :, 0:step, :], a[:, :, 0:step, :]).then_inc(s["run_s"], 1)
                dve.tensor_tensor(b[:, :, step:, :], a[:, :, step:, :], a[:, :, 0:NT + 1 - step, :], ALU.add).then_inc(s["run_s"], 1)
                ran += 2
                dve.wait_ge(s["run_s"], ran)
                now, step = 1 - now, 2 * step
            acc = run[now]
            dve.wait_ge(s["pref_mm"], 1)
            for h in range(2):
                dve.tensor_tensor(place[:, h], B_[:, 0, h * NT * E:(h + 1) * NT * E].rearrange("p (t e) -> p t e", e=E),
                                  acc[:, h, 0:NT, :], ALU.add).then_inc(s["place_s"], 1)
            dve.wait_ge(s["place_s"], 2)
            dve.tensor_tensor(place[:, 1], place[:, 1], acc[:, 0, NT:NT + 1, :].broadcast_to([P, NT, E]), ALU.add).then_inc(s["place_s"], 1)
            dve.wait_ge(s["place_s"], 3)
            for h in range(2):
                dve.scalar_tensor_tensor(place[:, h].rearrange("p t e -> p (t e)"), place[:, h].rearrange("p t e -> p (t e)"), NOWHERE,
                                         above[:, h].rearrange("p t e -> p (t e)"), ALU.subtract, ALU.mult).then_inc(s["pos_a"], 1)
            dve.wait_ge(s["pos_a"], 2)
            dve.scalar_tensor_tensor(pos[:].rearrange("p t e -> p (t e)"), place[:, 0].rearrange("p t e -> p (t e)"), NOWHERE,
                                     place[:, 1].rearrange("p t e -> p (t e)"), ALU.add, ALU.add).then_inc(s["pos_s"], 1)
            dve.wait_ge(s["pos_s"], 1)
            dve.tensor_scalar(loi[:], pos[:], P - 1, None, ALU.bitwise_and).then_inc(s["split_i"], 1)
            dve.tensor_scalar(hii[:], pos[:], int(math.log2(P)), None, ALU.logical_shift_right).then_inc(s["split_i"], 1)
            dve.wait_ge(s["split_i"], 2)
            dve.tensor_copy(lof[:], loi[:]).then_inc(s["split_f"], 1)
            dve.tensor_copy(hif[:], hii[:]).then_inc(s["split_f"], 1)
            dve.wait_ge(s["split_f"], 2)

            def places(e, first):
                if not first:
                    dve.wait_ge(s["id_mm"], e)
                dve.tensor_copy(lo_e[:], lof[:, :, bass.ds(e, 1)].rearrange("p t o -> p (t o)")).then_inc(s["lo_s"], 1)
                dve.tensor_tensor(inhi[:], iota8[:], hif[:, :, bass.ds(e, 1)].broadcast_to([P, NT, KT]), ALU.is_equal).then_inc(s["hi_s"], 1)
                dve.wait_ge(s["hi_s"], e + 1)
                dve.tensor_tensor(val[:, :, 0, :], inhi[:], tileno[:], ALU.mult).then_inc(s["val_s"], 1)
                dve.tensor_scalar(val[:, :, 1, :], inhi[:], partno[:, 0:1], None, ALU.mult).then_inc(s["val_s"], 1)
                dve.wait_ge(s["lo_s"], e + 1)

            def onehot(t0, t1):
                for t in range(t0, t1):
                    dve.tensor_scalar(oneh[:, t, :], iota16[:], lo_e[:, t:t + 1], None, ALU.is_equal).then_inc(s["hot_s"], 1)

            def read_list(e, first):
                dve.wait_ge(s["id_mm"], e + 1)
                if not first:
                    dve.wait_ge(s["ids_s_"], e)
                dve.tensor_copy(idp[:], D_[:, 0, 0:2 * KT].rearrange("p (a t) -> p a t", a=2)).then_inc(s["id_ev"], 1)

            def ids_of(e, first):
                dve.wait_ge(s["id_ev"], e + 1)
                if not first:
                    dve.wait_ge(s["idss_s"], e)
                dve.scalar_tensor_tensor(ids[:], idp[:, 0, :], float(P), idp[:, 1, :], ALU.mult, ALU.add).then_inc(s["ids_s_"], 1)

            def keep(e, first):
                dve.wait_ge(s["gat_a"], 8 * KT * (e + 1))
                dve.wait_ge(s["gat_b"], 8 * KT * (e + 1))
                if not first:
                    dve.wait_ge(s["y_o"], KT * e)
                    dve.wait_ge(s["sc_done"], 16 * KT * e)
                dve.tensor_copy(ids_s[:], ids[:]).then_inc(s["idss_s"], 1)
                dve.tensor_copy(ge[:], ex[:, :, bass.ds(D + e, 1)].rearrange("p t o -> p (t o)")).then_inc(s["ge_s"], 1)
                dve.tensor_copy(b2e[:], b2_bc[:, bass.ds(e, 1), :].rearrange("p o d -> p (o d)")).then_inc(s["b2e_s"], 1)

            def b1_of(e, first):
                if not first:
                    dve.wait_ge(s["h_hi"], 2 * FC * e)
                dve.tensor_copy(b1e[:], bcol[:, bass.ds(e * FC, FC)]).then_inc(s["b1e_s"], 1)

            def w1_lo(e, j):
                c, half = j // 2, slice((j % 2) * (FF // 2), (j % 2 + 1) * (FF // 2))
                dve.wait_ge(s["w1_hi_s"], DC * e + c + 1)
                dve.scalar_tensor_tensor(w1[1][:, c, half], w1r[:, c, half], FS, w1[0][:, c, half],
                                         ALU.mult, ALU.subtract).then_inc(s["w1_lo_s"], 1)

            def w2_split(e, j, first):
                rows = slice(j * (FC // 4), (j + 1) * (FC // 4))
                if j == 0:
                    dve.wait_ge(s["ld_w2"], 16 * (e + 1))
                    if not first:
                        dve.wait_ge(s["y_mm"], KT * e)
                dve.tensor_scalar(w2[0][:, rows], w2r[:, rows], FS, None, ALU.mult).then_inc(s["w2_hi_s"], 1)
                dve.wait_ge(s["w2_hi_s"], 4 * e + j + 1)
                dve.scalar_tensor_tensor(w2[1][:, rows], w2r[:, rows], FS, w2[0][:, rows],
                                         ALU.mult, ALU.subtract).then_inc(s["w2_lo_s"], 1)

            def ex_lo(e, i):
                dve.wait_ge(s["ex_hi"], 4 * e + i + 1)
                span = slice((i // 2) * 512, (i // 2 + 1) * 512)
                dve.scalar_tensor_tensor(exT[1][:, i % 2, span], D_[:, i % 2, :], XS, exT[0][:, i % 2, span],
                                         ALU.mult, ALU.subtract).then_inc(s["ex_lo"], 1)

            def expert(e, first, next1, next2):
                b1_of(e, first)
                if not first and next1:
                    read_list(e + 1, False)
                for u in range(2 * FC):
                    h, f = u // FC, u % FC
                    if first and u == SPLIT:
                        ex_lo(0, 2)
                        ex_lo(0, 3)
                    dve.wait_ge(s["h_hi"], 2 * FC * e + u + 1)
                    dve.tensor_tensor(hid[1][:, f, h * 512:(h + 1) * 512], g32[:, u % 2, :], hid[0][:, f, h * 512:(h + 1) * 512],
                                      ALU.subtract).then_inc(s["h_lo"], 1)
                    if u % 2 and u // 2 < 4:
                        w2_split(e, u // 2, first)
                    if u == KEEP:
                        keep(e, first)
                        if next1:
                            ids_of(e + 1, False)
                for t in range(KT):
                    dve.wait_ge(s["y_mm"], KT * e + t + 1)
                    if t == 0:
                        dve.wait_ge(s["b2e_s"], e + 1)
                    if not (first and t < 2):
                        dve.wait_ge(s["y_o"], KT * e + t - 1)
                    dve.scalar_tensor_tensor(yt[:, t % 2, :], C_[:, t % 2, 0:D], 1.0 / FS, b2e[:],
                                             ALU.mult, ALU.add).then_inc(s["y_t"], 1)
                    if next1 and t < 4:
                        w1_lo(e + 1, t)
                        ex_lo(e + 1, t)
                    if next2:
                        if t == 0:
                            places(e + 2, False)
                        elif t < KT - 1:
                            onehot(NT * (t - 1) // (KT - 2), NT * t // (KT - 2))

            places(0, True)
            onehot(0, NT)
            read_list(0, True)
            ids_of(0, True)
            places(1, False)
            onehot(0, NT)
            read_list(1, False)
            for j in range(4):
                w1_lo(0, j)
            for i in range(2):
                ex_lo(0, i)
            dve.wait_ge(s["ld_b2"], 16 * E)
            expert(0, True, True, True)
            with dve.Fori(1, E - 2) as e:
                expert(e, False, True, True)
            expert(E - 2, False, True, False)
            expert(E - 1, False, False, False)

        @block.tensor
        def _(pe):
            def pairs(out, lhs, rhs, chunks):
                terms = [(a, b, c) for c in range(chunks) for a, b in ((0, 0), (0, 1), (1, 0))]
                for i, (a, b, c) in enumerate(terms):
                    last = pe.matmul(out, lhs(a, c), rhs(b, c), start=i == 0, stop=i == len(terms) - 1)
                return last

            def transposes(out, src, tiles_, chunks):
                for t in range(tiles_):
                    for c in range(chunks):
                        last = pe.transpose(out[:, c, t * P:(t + 1) * P], src[:, t, c * P:(c + 1) * P], ident[:])
                return last

            wsp = [w_hi, w_lo]
            pe.wait_ge(s["const1"], 4)
            pe.wait_ge(s["xn_rdy"], TP)
            transposes(D_, xn, TP, DC).then_inc(s["x_tr"], 1)
            pe.wait_ge(s["ld_ctx"], 16)
            transposes(C_, ctx, TP, DC).then_inc(s["c_tr"], 1)
            pe.wait_ge(s["ld_b"], 48)
            NR = NB1 + 2 * DC
            pe.transpose(A_[:, 1, 0:NR], brow[:], ident[0:NR, 0:NR]).then_inc(s["b_tr"], 1)
            pe.wait_ge(s["w_lo_s"], 1)
            pe.wait_ge(s["ld_wg"], 16)
            pe.wait_ge(s["b_col"], 1)

            def body(n, k):
                if runs(n, k, 0):
                    pe.wait_ge(s["x_lo"], n + 1)
                    if k != 0:
                        pe.wait_ge(s["v_lo"], n)
                    for e in range(DC):
                        pairs(A_[:, e, :], lambda a, d: wsp[a][:, 0, d, e * P:(e + 1) * P],
                              lambda b, d: xT[b][:, d, :], DC).then_inc(s["q_mm"], 1)
                    pe.wait_ge(s["c_lo"], n + 1)
                    for e in range(DC):
                        pairs(D_[:, e, :], lambda a, d: wsp[a][:, 1, d, e * P:(e + 1) * P],
                              lambda b, d: cT[b][:, d, :], DC).then_inc(s["k_mm"], 1)
                if runs(n, k, 2):
                    pe.wait_ge(s["xn2_rdy"], TP * (n - 1))
                    if k != 2:
                        pe.wait_ge(s["l_ev"], n - 2)
                    transposes(C_, xn2, TP, DC).then_inc(s["x2_tr"], 1)
                if runs(n, k, 1):
                    pe.wait_ge(s["s_exp"], TP * n)
                    transposes(B_, prob, TP, SC).then_inc(s["p_tr"], 1)
                if runs(n, k, 0):
                    pe.wait_ge(s["q_lo"], DC * (n + 1))
                    for t in range(TP):
                        last = pairs(A_[:, t // 2, (t % 2) * D:(t % 2 + 1) * D], lambda a, d: cT[a][:, d, t * P:(t + 1) * P],
                                     lambda b, d: wsp[b][:, 2, d, :], DC)
                    last.then_inc(s["v_mm"], 1)
                if runs(n, k, 2):
                    pe.wait_ge(s["x2_ev"], n - 1)
                    for t in range(TP):
                        for d in range(DC):
                            last = pe.matmul(C_[:, 0, t * E:(t + 1) * E], xn2T[:, d, t * P:(t + 1) * P], wg[:, d, :],
                                             start=d == 0, stop=d == DC - 1)
                    last.then_inc(s["l_mm"], 1)
                if runs(n, k, 1):
                    pe.wait_ge(s["p_lo"], n)
                    pe.wait_ge(s["v_lo"], n)
                    for t in range(TP):
                        pairs(B_[:, t // 2, (t % 2) * D:(t % 2 + 1) * D], lambda a, c: pT[a][:, c, t * P:(t + 1) * P],
                              lambda b, c: v[b][:, (t // SC) * SC + c, :], SC).then_inc(s["o_mm"], 1)
                if runs(n, k, -1):
                    pe.wait_ge(s["xn_rdy"], TP * (n + 2))
                    pe.wait_ge(s["k_lo"], DC * (n + 1))
                    transposes(D_, xn, TP, DC).then_inc(s["x_tr"], 1)
                    pe.wait_ge(s["ld_ctx"], 16 * (n + 2))
                    if k is None or k >= 2:
                        pe.wait_ge(s["l_ev"], n - 1)
                    transposes(C_, ctx, TP, DC).then_inc(s["c_tr"], 1)
                if runs(n, k, 0):
                    pe.wait_ge(s["q_lo"], DC * (n + 1))
                    pe.wait_ge(s["k_lo"], DC * (n + 1))
                    if k != 0:
                        pe.wait_ge(s["o_ev"], TP * n)
                    for t in range(TP):
                        b0 = (t // SC) * S
                        last = pairs(B_[:, t // 2, (t % 2) * S:(t % 2 + 1) * S], lambda a, e: qT[a][:, e, t * P:(t + 1) * P],
                                     lambda b, e: kT[b][:, e, b0:b0 + S], DC)
                    last.then_inc(s["s_mm"], 1)

            phase_a(pe, body)

            pe.wait_ge(s["gate_r"], 1)
            for h in range(2):
                last = pe.transpose(A_[:, 0, h * P:(h + 1) * P], gate[:, h * HT:(h + 1) * HT, :].rearrange("p t e -> p (t e)"), ident[:])
            last.then_inc(s["key_tr"], 1)
            pe.wait_ge(s["same_s"], 1)
            with pe.Fori(0, ROUNDS) as r:
                pe.wait_ge(s["srch_cmp"], 3 * (r + 1))
                pe.matmul(A_[:, 1, 0:3], same16[:], cnt[:], start=True, stop=True).then_inc(s["srch_mm"], 1)
            pe.wait_ge(s["kq_s"], 1)
            pe.wait_ge(s["key_ev"], 1)
            pe.matmul(A_[:, 0, 0:E], onesf[:], kth_q[:], start=True, stop=True).then_inc(s["kq_mm"], 1)
            pe.wait_ge(s["above_s"], 2)
            flags = above[:].rearrange("p a t e -> p (a t e)")
            pe.matmul(C_[:, 0, :], ones16[:], flags, start=True, stop=True).then_inc(s["tot_mm"], 1)
            pe.matmul(B_[:, 0, :], before16[:], flags, start=True, stop=True).then_inc(s["pref_mm"], 1)

            def list_of(e, first):
                pe.wait_ge(s["val_s"], 2 * (e + 1))
                if not first:
                    pe.wait_ge(s["id_ev"], e)
                for t in range(NT):
                    if t % 8 == 0:
                        pe.wait_ge(s["hot_s"], NT * e + t + 8)
                    last = pe.matmul(D_[:, 0, 0:2 * KT], oneh[:, t, :], val[:, t].rearrange("p a j -> p (a j)"),
                                     start=t == 0, stop=t == NT - 1)
                last.then_inc(s["id_mm"], 1)

            def rows_T(e, i):
                pe.wait_ge(s["gat_a"] if i < 2 else s["gat_b"], 8 * KT * (e + 1))
                if i >= 2:
                    pe.wait_ge(s["ex_lo"], 4 * e + i - 1)
                for j in range(4):
                    last = pe.transpose(D_[:, i % 2, j * P:(j + 1) * P], ex[:, (i // 2) * 4 + j, (i % 2) * P:(i % 2 + 1) * P], ident[:])
                last.then_inc(s["ex_tr"], 1)

            def expert(e, first, next1, next2):
                pe.wait_ge(s["w1_lo_s"], 4 * (e + 1))
                for u in range(2 * FC):
                    h, f = u // FC, u % FC
                    if first and u == SPLIT:
                        rows_T(0, 2)
                        rows_T(0, 3)
                    if f == 0:
                        pe.wait_ge(s["ex_lo"], 4 * e + 2 * (h + 1))
                    if not (first and u < 4):
                        pe.wait_ge(s["h_hi"], 2 * FC * e + u - 3)
                    pairs(bank[(u % 4) // 2][:, u % 2, :], lambda a, c: w1[a][:, c, f * P:(f + 1) * P],
                          lambda b, c: exT[b][:, c, h * 512:(h + 1) * 512], DC).then_inc(s["h_mm"], 1)
                pe.wait_ge(s["w2_lo_s"], 4 * (e + 1))
                for t in range(KT):
                    if t % (KT // 2) == 0:
                        pe.wait_ge(s["h_lo"], 2 * FC * e + FC * (t // (KT // 2) + 1))
                    if not (first and t < 2):
                        pe.wait_ge(s["y_t"], KT * e + t - 1)
                    pairs(C_[:, t % 2, 0:D], lambda a, f: hid[a][:, f, t * P:(t + 1) * P],
                          lambda b, f: w2[b][:, f, :], FC).then_inc(s["y_mm"], 1)
                    if next1 and t < 4:
                        if t == 0:
                            pe.wait_ge(s["id_ev"], e + 2)
                        rows_T(e + 1, t)
                if next2:
                    pe.wait_ge(s["ex_lo"], 4 * (e + 2))
                    list_of(e + 2, False)

            pe.wait_ge(s["l_ev"], NP)
            list_of(0, True)
            list_of(1, False)
            pe.wait_ge(s["id_ev"], 2)
            for i in range(2):
                rows_T(0, i)
            expert(0, True, True, True)
            with pe.Fori(1, E - 2) as e:
                expert(e, False, True, True)
            expert(E - 2, False, True, False)
            expert(E - 1, False, False, False)


INS = ["x", "ctx_1024", "L0_xattn_Wq", "L0_xattn_bq", "L0_xattn_Wk", "L0_xattn_bk", "L0_xattn_Wv", "L0_xattn_bv",
       "L0_ffn_Wg", "L0_ffn_W1", "L0_ffn_b1", "L0_ffn_W2", "L0_ffn_b2"]


def kernel(**inputs):
    import concourse.bacc as bacc
    from concourse.bass_utils import run_bass_kernel_spmd

    nc = bacc.Bacc("TRN2", target_bir_lowering=False, num_devices=1)
    arrays, args = {}, []
    for name in INS:
        a = np.ascontiguousarray(inputs[name])
        arrays[f"in_{name}"] = a
        args.append(nc.dram_tensor(f"in_{name}", a.shape, mybir.dt.from_np(a.dtype), kind="ExternalInput").ap())
    out = nc.dram_tensor("out", inputs["x"].shape, F32, kind="ExternalOutput").ap()
    build(nc, *args, out)
    r = run_bass_kernel_spmd(nc, [arrays], core_ids=[0])
    return r.results[0]["out"]
```

```python
import math
from contextlib import ExitStack

import numpy as np
import concourse.bass as bass
from concourse import mybir

F32 = mybir.dt.float32
F16 = mybir.dt.float16
BF16 = mybir.dt.bfloat16
I32 = mybir.dt.int32
ALU = mybir.AluOpType
ACT = mybir.ActivationFunctionType
AX = mybir.AxisListType

P = 128


def build(nc, x_d, ctx_d, wq_d, bq_d, wk_d, bk_d, wv_d, bv_d, wg_d, w1_d, b1_d, w2_d, b2_d, out_d):
    B, S, D = x_d.shape
    E, _, FF = w1_d.shape
    N = B * S
    K = max(N * 2 // E, 1)
    NT = N // P
    TP = 4
    NP = NT // TP
    PAIR = TP * P
    DC = D // P
    FC = FF // P
    KT = K // P
    SC = S // P
    EPS = 1e-5

    XS = 4.0
    AS = 16.0
    QS = XS * AS
    PS = 4096.0
    FS = 256.0
    SCORE = 1.0 / (QS * QS * math.sqrt(D))
    BITS = 30
    ROUNDS = BITS // 2
    UNROLL = 5
    HOTS = 4
    KEEP = 5
    SPLIT = 1
    NOWHERE = float(N)

    with ExitStack() as stack:
        def sb(name, shape, dt=F32):
            return stack.enter_context(nc.sbuf_tensor(name, shape, dt))

        def sem(name):
            return stack.enter_context(nc.semaphore(name))

        rows_d = nc.dram_tensor("rows_d", [N, D + E], F32).ap()

        ident = sb("ident", [P, P])
        before16 = sb("before16", [P, P], BF16)
        same16 = sb("same16", [P, P], BF16)
        apart = sb("apart", [P, P], I32)
        onesf = sb("onesf", [P, P])
        pick = sb("pick", [P, E])
        order16 = sb("order16", [P, 4, P], BF16)
        iota16 = sb("iota16", [P, P, NT], BF16)
        iota8 = sb("iota8", [P, NT, KT])
        tileno = sb("tileno", [P, NT, KT])
        partno = sb("partno", [P, 1])
        mhalf = sb("mhalf", [P, TP])
        eps = sb("eps", [P, TP]); minus = sb("minus", [P, TP])
        act_tick = sb("act_tick", [P, 1]); dve_tick = sb("dve_tick", [P, 4]); pool_tick = sb("pool_tick", [P, KT + 1])
        w_raw = sb("w_raw", [P, 3, DC, D])
        w_hi = sb("w_hi", [P, 3, DC, D], F16)
        w_lo = sb("w_lo", [P, 3, DC, D], F16)
        wg = sb("wg", [P, DC, E])
        NB1 = E * FC
        brow = sb("brow", [NB1 + 2 * DC, P])
        bcol = sb("bcol", [P, NB1 + 2 * DC])
        bqk = sb("bqk", [P, 2 * DC])
        bv_bc = sb("bv_bc", [P, TP, D])
        b2_bc = sb("b2_bc", [P, E, D])
        xres = sb("xres", [P, NT, D])
        ctx = sb("ctx", [P, TP, D])
        xn = sb("xn", [P, TP, D])
        xn2 = sb("xn2", [P, TP, D])
        st1 = sb("st1", [P, TP, 6]); mv1 = sb("mv1", [P, TP, 2])
        rstd1 = sb("rstd1", [P, TP]); nmr1 = sb("nmr1", [P, TP])
        st2 = sb("st2", [P, TP, 6]); mv2 = sb("mv2", [P, TP, 2])
        rstd2 = sb("rstd2", [P, TP]); nmr2 = sb("nmr2", [P, TP])
        xT = [sb(f"xT{i}", [P, DC, PAIR], F16) for i in "hl"]
        cT = [sb(f"cT{i}", [P, DC, PAIR], F16) for i in "hl"]
        qT = [sb(f"qT{i}", [P, DC, PAIR], F16) for i in "hl"]
        kT = [sb(f"kT{i}", [P, DC, PAIR], F16) for i in "hl"]
        v = [sb(f"v{i}", [P, TP, D], F16) for i in "hl"]
        prob = sb("prob", [P, TP, S])
        pT = [sb(f"pT{i}", [P, SC, PAIR], F16) for i in "hl"]
        nmax = sb("nmax", [P, TP]); nbias = sb("nbias", [P, TP])
        rsum = sb("rsum", [P, TP]); rinv = sb("rinv", [P, TP]); rinvs = sb("rinvs", [P, TP])
        xn2T = sb("xn2T", [P, DC, PAIR])
        logit = sb("logit", [P, NT, E])
        gate = sb("gate", [P, NT, E])
        HT = NT // 2
        keyT = sb("keyT", [P, 2, P])
        junk = sb("junk", [P, 4, 2, P], BF16)
        steps = sb("steps", [P, 3], I32)
        trial = sb("trial", [P, 3], I32)
        cand = sb("cand", [P, 4])
        cnt = sb("cnt", [P, 3], BF16)
        kth_q = sb("kth_q", [P, E])
        above = sb("above", [P, 2, NT, E], BF16)
        tot = sb("tot", [P, 2, 2], BF16)
        place = sb("place", [P, 2, NT, E])
        pos = sb("pos", [P, NT, E], I32)
        loi = sb("loi", [P, NT, E], I32); hii = sb("hii", [P, NT, E], I32)
        lo_e = sb("lo_e", [P, NT], BF16)
        hi_e = sb("hi_e", [P, NT])
        oneh = sb("oneh", [P, P, NT], BF16)
        inhi = sb("inhi", [P, NT, KT])
        val = sb("val", [P, NT, 2, KT], BF16)
        idp = sb("idp", [P, 2, KT])
        ids = sb("ids", [P, KT], I32)
        ids_s = sb("ids_s", [P, KT], I32)
        ex = sb("ex", [P, KT, D + E])
        ge = sb("ge", [P, KT])
        exT = [sb(f"exT{i}", [P, DC, K], F16) for i in "hl"]
        w1r = sb("w1r", [P, DC, FF]); w2r = sb("w2r", [P, FC, D])
        w1 = [sb(f"w1{i}", [P, DC, FF], F16) for i in "hl"]
        w2 = [sb(f"w2{i}", [P, FC, D], F16) for i in "hl"]
        b1e = sb("b1e", [P, FC])
        b2e = sb("b2e", [P, D])
        g32 = sb("g32", [P, 2, PAIR])
        hid = [xres[:, i * NT // 2:(i + 1) * NT // 2, :].bitcast(F16).rearrange("p t d -> p (t d)")
               .rearrange("p (f k) -> p f k", f=FC) for i in range(2)]
        yt = sb("yt", [P, 2, D])
        yo = sb("yo", [P, KT, D])

        bank = [stack.enter_context(nc.psum_tensor(f"bank{i}", [P, 2, 512], F32)) for i in range(4)]
        A_, B_, C_, D_ = bank

        names = """ld_x0 ld_x1 ld_x2 ld_w ld_wg ld_b ld_bv ld_b2 ld_ctx const0 const1 const2 const3 and_s same_s
            w_hi_s w_lo_s b_tr b_col b_qk
            ln1_st ln1_mv ln1_eps ln1_rstd ln1_mr ln1_nmr xn_rdy xbv
            x_tr x_hi x_lo c_tr c_hi c_lo q_mm q_hi q_lo k_mm k_hi k_lo v_mm v_hi v_lo
            s_mm s_max s_nb s_exp s_ri s_ris p_tr p_hi p_lo o_mm o_ev
            ln2_st ln2_mv ln2_eps ln2_rstd ln2_mr ln2_nmr xn2_rdy st_x1 st_xn
            x2_tr x2_ev l_mm l_ev
            gate_r st_gate key_tr key_ev init_s srch_tr srch_cmp srch_mm srch_sel srch_base srch_step
            kq_s kq_mm above_s tot_s pref_mm pos_a pos_s split_i early_s
            lo_s hot_s hie_s hi_s val_s id_mm id_ev list_rdy list_kept gat_a gat_b ge_s ex_tr ex_hi ex_lo
            ld_w1 ld_w2 w1_hi_s w1_lo_s w2_hi_s w2_lo_s b1e_s b2e_s
            h_mm h_hi h_lo y_mm y_t y_o sc_done tick_g tick_s""".split()
        s = {n: sem(n) for n in names}

        block = stack.enter_context(nc.Block())
        MID0, MID1 = 3, NP - 3

        def phase_a(engine, body):
            for n in range(MID0):
                body(n, n)
            with engine.Fori(MID0, MID1 + 1) as n:
                body(n, None)
            for n in range(MID1 + 1, NP + 2):
                body(n, n)

        def runs(n, k, shift):
            return k is None or 0 <= k - shift < NP

        def half(a, h):
            return a[:, :, h * 2 * P:(h + 1) * 2 * P]

        def by_half(b, h):
            return b[:, h, :].rearrange("p (c k) -> p c k", c=2)

        def tiles(n):
            return bass.ds(n * TP, TP)

        @block.sync
        def _(sp):
            xv = x_d.rearrange("b (c p) d -> p (b c) d", p=P)
            cv = ctx_d.rearrange("b (c p) d -> p (b c) d", p=P)
            ov = out_d.rearrange("b (c p) d -> p (b c) d", p=P)
            rv = rows_d.rearrange("(t p) d -> p t d", p=P)
            sp.dma_start(xres[:, 0:TP, :], xv[:, 0:TP, :]).then_inc(s["ld_x0"], 16)
            sp.dma_start(ctx[:, :, :], cv[:, 0:TP, :]).then_inc(s["ld_ctx"], 16)
            for i, w_d in enumerate((wq_d, wk_d, wv_d)):
                sp.dma_start(w_raw[:, i], w_d.rearrange("(c p) e -> p c e", p=P)).then_inc(s["ld_w"], 16)
            sp.dma_start(brow[0:NB1, :], b1_d.rearrange("e (f p) -> (e f) p", p=P)).then_inc(s["ld_b"], 16)
            sp.dma_start(brow[NB1:NB1 + DC, :], bq_d.rearrange("(f p) -> f p", p=P)).then_inc(s["ld_b"], 16)
            sp.dma_start(brow[NB1 + DC:NB1 + 2 * DC, :], bk_d.rearrange("(f p) -> f p", p=P)).then_inc(s["ld_b"], 16)
            sp.dma_start(xres[:, TP:2 * TP, :], xv[:, TP:2 * TP, :]).then_inc(s["ld_x1"], 16)
            for t in range(TP):
                sp.dma_start(bv_bc[:, t, :], bv_d.partition_broadcast(P)).then_inc(s["ld_bv"], 16)
            sp.dma_start(wg[:, :, :], wg_d.rearrange("(c p) e -> p c e", p=P)).then_inc(s["ld_wg"], 16)

            def body(n, k):
                if runs(n, k, -1):
                    sp.wait_ge(s["c_tr"], n + 1)
                    sp.dma_start(ctx[:, :, :], cv[:, tiles(n + 1), :]).then_inc(s["ld_ctx"], 16)
                if k == 0:
                    sp.dma_start(xres[:, 2 * TP:NT, :], xv[:, 2 * TP:NT, :]).then_inc(s["ld_x2"], 16)
                if k == 1:
                    for e in range(E):
                        sp.dma_start(b2_bc[:, e, :], b2_d[e, :].partition_broadcast(P)).then_inc(s["ld_b2"], 16)
                    sp.dma_start(w1r[:, :, :], w1_d[0].rearrange("(c p) f -> p c f", p=P)).then_inc(s["ld_w1"], 16)
                    sp.dma_start(w2r[:, :, :], w2_d[0].rearrange("(c p) f -> p c f", p=P)).then_inc(s["ld_w2"], 16)
                if runs(n, k, 2):
                    sp.wait_ge(s["xn2_rdy"], TP * (n - 1))
                    sp.dma_start(rv[:, tiles(n - 2), 0:D], xn2[:, :, :]).then_inc(s["st_xn"], 16)
                if runs(n, k, 1):
                    sp.wait_ge(s["o_ev"], TP * n)
                    sp.dma_start(ov[:, tiles(n - 1), :], xres[:, tiles(n - 1), :]).then_inc(s["st_x1"], 16)

            phase_a(sp, body)
            sp.wait_ge(s["gate_r"], 1)
            sp.dma_start(rv[:, :, D:D + E], gate[:, :, :]).then_inc(s["st_gate"], 16)
            with sp.Fori(1, E) as e:
                sp.wait_ge(s["w1_lo_s"], 4 * e)
                sp.dma_start(w1r[:, :, :], w1_d[bass.ds(e, 1)].rearrange("o (c p) f -> p (o c) f", p=P)).then_inc(s["ld_w1"], 16)
                sp.wait_ge(s["w2_lo_s"], 4 * e)
                sp.dma_start(w2r[:, :, :], w2_d[bass.ds(e, 1)].rearrange("o (c p) f -> p (o c) f", p=P)).then_inc(s["ld_w2"], 16)
            sp.wait_ge(s["sc_done"], 16 * KT * E)
            sp.wait_ge(s["st_x1"], 16 * NP)
            sp.wait_ge(s["st_xn"], 16 * NP)
            sp.wait_ge(s["st_gate"], 16)

        @block.gpsimd
        def _(pool):
            pool.memset(ident[:], 0.0).then_inc(s["const0"], 1)
            pool.memset(before16[:], 1.0).then_inc(s["const0"], 1)
            pool.memset(pick[:], 0.0).then_inc(s["const0"], 1)
            pool.wait_ge(s["const0"], 3)
            pool.affine_select(out=ident[:], in_=ident[:], compare_op=ALU.not_equal, fill=1.0, base=0,
                               pattern=[[-1, P]], channel_multiplier=1).then_inc(s["const1"], 1)
            pool.affine_select(out=before16[:], in_=before16[:], compare_op=ALU.is_gt, fill=0.0, base=0,
                               pattern=[[1, P]], channel_multiplier=-1).then_inc(s["const1"], 1)
            pool.affine_select(out=pick[:], in_=pick[:], compare_op=ALU.not_equal, fill=1.0, base=0,
                               pattern=[[-1, E]], channel_multiplier=1).then_inc(s["const1"], 1)
            pool.memset(mhalf[:], -0.5).then_inc(s["const1"], 1)
            pool.memset(eps[:], EPS).then_inc(s["const1"], 1)
            pool.memset(minus[:], -1.0).then_inc(s["const1"], 1)
            pool.memset(onesf[:], 1.0).then_inc(s["const1"], 1)

            def ln_scale(mv, rstd, nmr, a, c, tl):
                pool.tensor_tensor(rstd[:, tl], mv[:, tl, 1], eps[:, tl], ALU.add).then_inc(s[a + "_eps"], 1)
                pool.wait_ge(s[a + "_eps"], c + 1)
                pool.tensor_tensor(rstd[:, tl], rstd[:, tl], mhalf[:, tl], ALU.pow).then_inc(s[a + "_rstd"], 1)
                pool.wait_ge(s[a + "_rstd"], c + 1)
                pool.tensor_tensor(nmr[:, tl], mv[:, tl, 0], rstd[:, tl], ALU.mult).then_inc(s[a + "_mr"], 1)
                pool.wait_ge(s[a + "_mr"], c + 1)
                pool.tensor_tensor(nmr[:, tl], nmr[:, tl], minus[:, tl], ALU.mult).then_inc(s[a + "_nmr"], 1)

            def ln1(n, first=False):
                for h in range(2):
                    pool.wait_ge(s["ln1_mv"], TP * n + 2 * h + 2)
                    if not first and h == 0:
                        pool.wait_ge(s["xn_rdy"], TP * n)
                    ln_scale(mv1, rstd1, nmr1, "ln1", 2 * n + h, slice(2 * h, 2 * h + 2))

            def add_bv(n):
                pool.wait_ge(s["xn_rdy"], TP * (n + 1))
                pool.tensor_tensor(xres[:, tiles(n), :], xres[:, tiles(n), :], bv_bc[:], ALU.add).then_inc(s["xbv"], 1)

            pool.wait_ge(s["const1"], 6)
            ln1(0, True)
            pool.wait_ge(s["ld_bv"], 16 * TP)
            add_bv(0)

            def body(n, k):
                if runs(n, k, -1):
                    ln1(n + 1)
                    add_bv(n + 1)
                if runs(n, k, 1):
                    for h in range(2):
                        pool.wait_ge(s["ln2_mv"], TP * (n - 1) + 2 * h + 2)
                        if k != 1 and h == 0:
                            pool.wait_ge(s["xn2_rdy"], TP * (n - 1))
                        ln_scale(mv2, rstd2, nmr2, "ln2", 2 * (n - 1) + h, slice(2 * h, 2 * h + 2))
                if k == 1:
                    pool.iota(apart[:], [[1, P]], base=P, channel_multiplier=-1).then_inc(s["const2"], 1)
                    pool.iota(iota8[:], [[0, NT], [1, KT]], base=0, channel_multiplier=0,
                              allow_small_or_imprecise_dtypes=True).then_inc(s["const2"], 1)
                    pool.iota(tileno[:], [[1, NT], [0, KT]], base=0, channel_multiplier=0,
                              allow_small_or_imprecise_dtypes=True).then_inc(s["const2"], 1)
                    pool.iota(partno[:], [[0, 1]], base=0, channel_multiplier=1,
                              allow_small_or_imprecise_dtypes=True).then_inc(s["const2"], 1)

            phase_a(pool, body)
            pool.iota(iota16[:], [[1, P], [0, NT]], base=0, channel_multiplier=0,
                      allow_small_or_imprecise_dtypes=True).then_inc(s["const3"], 1)

            rows_out = out_d.rearrange("b s d -> (b s) d")

            def gather(e, first):
                pool.wait_ge(s["list_rdy"], e + 1)
                if not first:
                    pool.wait_ge(s["ex_tr"], 4 * e)
                    pool.wait_ge(s["ge_s"], e)
                    pool.wait_ge(s["tick_g"], e)
                pool.tensor_tensor(pool_tick[:, 0:1], eps[:, 0:1], eps[:, 0:1], ALU.add).then_inc(s["tick_g"], 1)
                for t in range(KT):
                    pool.indirect_dma_start(out=ex[:, t, :], out_offset=None, in_=rows_d,
                                            in_offset=bass.IndirectOffsetOnAxis(ap=ids[:, t:t + 1], axis=0)
                                            ).then_inc(s["gat_a"] if t < KT // 2 else s["gat_b"], 16)

            def scatter(e, first):
                if not first:
                    pool.wait_ge(s["sc_done"], 16 * KT * e)
                for t in range(KT):
                    pool.wait_ge(s["y_o"], KT * e + t + 1)
                    if not first:
                        pool.wait_ge(s["tick_s"], KT * (e - 1) + t + 1)
                    pool.tensor_tensor(pool_tick[:, t + 1:t + 2], eps[:, 0:1], eps[:, 0:1], ALU.add).then_inc(s["tick_s"], 1)
                    pool.indirect_dma_start(out=rows_out, out_offset=bass.IndirectOffsetOnAxis(ap=ids_s[:, t:t + 1], axis=0),
                                            in_=yo[:, t, :], in_offset=None, compute_op=ALU.add).then_inc(s["sc_done"], 16)

            pool.wait_ge(s["st_xn"], 16 * NP)
            pool.wait_ge(s["st_gate"], 16)
            gather(0, True)
            pool.wait_ge(s["st_x1"], 16 * NP)
            gather(1, False)
            scatter(0, True)
            with pool.Fori(1, E - 1) as e:
                gather(e + 1, False)
                scatter(e, False)
            scatter(E - 1, False)

        @block.scalar
        def _(act):
            def hi(dst, src, mm, done, count, scale=1.0, bias=0.0, func=ACT.Identity):
                act.wait_ge(s[mm], count)
                act.activation(dst, src, func, bias=bias, scale=scale).then_inc(s[done], 1)

            def apply_ln(dst, rstd, nmr, a, n, done):
                for t in range(TP):
                    if t % 2 == 0:
                        act.wait_ge(s[a + "_nmr"], 2 * n + t // 2 + 1)
                    act.activation(dst[:, t, :], xres[:, bass.ds(n * TP + t, 1), :].rearrange("p o d -> p (o d)"), ACT.Identity,
                                   bias=nmr[:, t:t + 1], scale=rstd[:, t:t + 1]).then_inc(s[done], 1)

            def w1_hi(e, c):
                act.activation(w1[0][:, c], w1r[:, c], ACT.Copy, scale=FS).then_inc(s["w1_hi_s"], 1)

            apply_ln(xn, rstd1, nmr1, "ln1", 0, "xn_rdy")
            act.wait_ge(s["ld_w"], 48)
            act.activation(w_hi[:], w_raw[:], ACT.Copy, scale=AS).then_inc(s["w_hi_s"], 1)
            hi(xT[0][:], D_[:], "x_tr", "x_hi", 1, scale=XS)
            act.wait_ge(s["b_tr"], 1)
            act.activation(bcol[:], A_[:, 1, 0:NB1 + 2 * DC], ACT.Copy).then_inc(s["b_col"], 1)
            hi(cT[0][:], C_[:], "c_tr", "c_hi", 1, scale=XS)
            act.wait_ge(s["b_qk"], 1)

            def x1_ln(n, k):
                if k != 2:
                    act.wait_ge(s["x2_tr"], 2 * (n - 2))
                    act.wait_ge(s["st_xn"], 16 * (n - 2))
                apply_ln(xn2, rstd2, nmr2, "ln2", n - 2, "xn2_rdy")

            def body(n, k):
                if runs(n, k, 0):
                    for c in range(DC):
                        act.wait_ge(s["q_mm"], DC * n + c + 1)
                        if k != 0 and c == 0:
                            act.wait_ge(s["s_mm"], 2 * n)
                        act.activation(qT[0][:, c, :], A_[:, c, :], ACT.Identity, bias=bqk[:, c:c + 1]).then_inc(s["q_hi"], 1)
                    for c in range(DC):
                        act.wait_ge(s["k_mm"], DC * n + c + 1)
                        act.activation(kT[0][:, c, :], D_[:, c, :], ACT.Identity, bias=bqk[:, DC + c:DC + c + 1]).then_inc(s["k_hi"], 1)
                if runs(n, k, 1):
                    if k != 1:
                        act.wait_ge(s["o_mm"], TP * (n - 1))
                    for h in range(2):
                        hi(half(pT[0], h), by_half(B_, h), "p_tr", "p_hi", 2 * (n - 1) + h + 1)
                if runs(n, k, 2):
                    x1_ln(n, k)
                if runs(n, k, -1):
                    act.wait_ge(s["x_tr"], n + 1)
                    apply_ln(xn, rstd1, nmr1, "ln1", n + 1, "xn_rdy")
                if runs(n, k, 0):
                    act.wait_ge(s["v_mm"], n + 1)
                    if k != 0:
                        act.wait_ge(s["o_mm"], TP * n)
                    act.activation(v[0][:], A_[:].rearrange("p a (b d) -> p (a b) d", d=D), ACT.Identity).then_inc(s["v_hi"], 1)
                if runs(n, k, 2):
                    for h in range(2):
                        act.wait_ge(s["x2_tr"], 2 * (n - 2) + h + 1)
                        if k != 2 and h == 0:
                            act.wait_ge(s["l_mm"], 2 * (n - 2))
                        act.activation(half(xn2T, h), by_half(C_, h), ACT.Copy).then_inc(s["x2_ev"], 1)
                if runs(n, k, -1):
                    hi(xT[0][:], D_[:], "x_tr", "x_hi", n + 2, scale=XS)
                    hi(cT[0][:], C_[:], "c_tr", "c_hi", n + 2, scale=XS)
                if k == NP:
                    act.wait_ge(s["ld_w1"], 16)
                    for c in range(DC):
                        w1_hi(0, c)
                if runs(n, k, 0):
                    if k != 0:
                        act.wait_ge(s["p_tr"], 2 * n)
                        act.wait_ge(s["s_ri"], n)
                    for t in range(TP):
                        if t % 2 == 0:
                            act.wait_ge(s["s_nb"], 2 * n + t // 2 + 1)
                        act.activation(prob[:, t, :], B_[:, t // 2, (t % 2) * S:(t % 2 + 1) * S], ACT.Exp,
                                       bias=nbias[:, t:t + 1], scale=SCORE,
                                       accum_out=rsum[:, t:t + 1]).then_inc(s["s_exp"], 1)

            phase_a(act, body)
            act.wait_ge(s["l_ev"], NP)
            act.activation(gate[:], logit[:], ACT.Sigmoid).then_inc(s["gate_r"], 1)
            act.wait_ge(s["key_tr"], 1)
            act.activation(keyT[:], A_[:, 0, 0:2 * P].rearrange("p (a b) -> p a b", a=2), ACT.Sigmoid).then_inc(s["key_ev"], 1)

            def ex_hi(e, i):
                act.wait_ge(s["ex_tr"], 4 * e + i + 1)
                act.activation(exT[0][:, i % 2, (i // 2) * 512:(i // 2 + 1) * 512], D_[:, i % 2, :],
                               ACT.Copy, scale=XS).then_inc(s["ex_hi"], 1)

            def layer1(e, first):
                act.wait_ge(s["b1e_s"], e + 1)
                if first:
                    act.activation(act_tick[:], eps[:, 0:1], ACT.Gelu)
                for u in range(2 * FC):
                    h, f = u // FC, u % FC
                    if first and u == SPLIT:
                        ex_hi(0, 2)
                        ex_hi(0, 3)
                    act.wait_ge(s["h_mm"], 2 * FC * e + u + 1)
                    src = bank[(u % 4) // 2][:, u % 2, :]
                    if not (first and u < 2):
                        act.wait_ge(s["h_lo"], 2 * FC * e + u - 1)
                    act.activation(g32[:, u % 2, :], src, ACT.Gelu, bias=b1e[:, f:f + 1],
                                   scale=1.0 / (XS * FS))
                    if not first and f == 0:
                        act.wait_ge(s["y_mm"], KT * (e - 1) + (KT // 2) * (h + 1))
                    act.activation(hid[0][:, f, h * 512:(h + 1) * 512], src, ACT.Gelu, bias=b1e[:, f:f + 1],
                                   scale=1.0 / (XS * FS)).then_inc(s["h_hi"], 1)

            def layer2(e, first, last):
                act.wait_ge(s["ge_s"], e + 1)
                if not first:
                    act.wait_ge(s["sc_done"], 16 * KT * e)
                if not last:
                    act.wait_ge(s["ld_w1"], 16 * (e + 2))
                for t in range(KT):
                    if not last and t < DC:
                        w1_hi(e + 1, t)
                    act.wait_ge(s["y_t"], KT * e + t + 1)
                    act.activation(yo[:, t, :], yt[:, t % 2, :], ACT.Copy, scale=ge[:, t:t + 1]).then_inc(s["y_o"], 1)
                    if not last and t < 4:
                        ex_hi(e + 1, t)

            for i in range(2):
                ex_hi(0, i)
            act.wait_ge(s["st_x1"], 16 * NP)
            layer1(0, True)
            layer2(0, True, False)
            with act.Fori(1, E - 1) as e:
                layer1(e, False)
                layer2(e, False, False)
            layer1(E - 1, False)
            layer2(E - 1, False, True)

        @block.vector
        def _(dve):
            def stats(n, st, mv, a, h):
                dve.memset(dve_tick[:, 2 * h:2 * h + 1], 0.0)
                for t in (2 * h, 2 * h + 1):
                    dve.bn_stats(st[:, t, :], xres[:, bass.ds(n * TP + t, 1), :].rearrange("p o d -> p (o d)")).then_inc(s[a + "_st"], 1)
                dve.wait_ge(s[a + "_st"], TP * n + 2 * h + 2)
                dve.memset(dve_tick[:, 2 * h + 1:2 * h + 2], 0.0)
                for t in (2 * h, 2 * h + 1):
                    dve.bn_aggr(mv[:, t, :], st[:, t, :]).then_inc(s[a + "_mv"], 1)

            def lo(dst, src, hi_, ready, count, done, scale=None):
                dve.wait_ge(s[ready], count)
                if scale is None:
                    dve.tensor_tensor(dst, src, hi_, ALU.subtract).then_inc(s[done], 1)
                else:
                    dve.scalar_tensor_tensor(dst, src, scale, hi_, ALU.mult, ALU.subtract).then_inc(s[done], 1)

            def w1_lo(e, j):
                c, cols = j // 2, slice((j % 2) * (FF // 2), (j % 2 + 1) * (FF // 2))
                dve.wait_ge(s["w1_hi_s"], DC * e + c + 1)
                dve.scalar_tensor_tensor(w1[1][:, c, cols], w1r[:, c, cols], FS, w1[0][:, c, cols],
                                         ALU.mult, ALU.subtract).then_inc(s["w1_lo_s"], 1)

            def search_constants():
                dve.wait_ge(s["const2"], 4)
                dve.tensor_scalar(apart[:], apart[:], E - 1, None, ALU.bitwise_and).then_inc(s["and_s"], 1)
                dve.wait_ge(s["and_s"], 1)
                dve.tensor_scalar(same16[:], apart[:], 0.0, None, ALU.is_equal).then_inc(s["same_s"], 1)
                dve.wait_ge(s["same_s"], 1)
                dve.wait_ge(s["const1"], 7)
                dve.tensor_tensor(order16[:, 0], same16[:], before16[:], ALU.mult).then_inc(s["early_s"], 1)
                dve.tensor_copy(order16[:, 1:4], same16[:, :].unsqueeze(1).broadcast_to([P, 3, P])).then_inc(s["early_s"], 1)
                for c in range(3):
                    dve.memset(steps[:, c:c + 1], (c + 1) << (BITS - 2)).then_inc(s["init_s"], 1)
                    dve.memset(trial[:, c:c + 1], (c + 1) << (BITS - 2)).then_inc(s["init_s"], 1)
                dve.memset(cand[:, 3:4], 0.0).then_inc(s["srch_tr"], 1)

            dve.wait_ge(s["ld_x0"], 16)
            for h in range(2):
                stats(0, st1, mv1, "ln1", h)
            lo(*(w[:].rearrange("p a b c -> p (a b c)") for w in (w_lo, w_raw, w_hi)), "w_hi_s", 1, "w_lo_s", AS)
            lo(xT[1][:], D_[:], xT[0][:], "x_hi", 1, "x_lo", XS)
            dve.wait_ge(s["b_col"], 1)
            dve.tensor_scalar(bqk[:], bcol[:, NB1:], QS, None, ALU.mult).then_inc(s["b_qk"], 1)
            dve.wait_ge(s["b_qk"], 1)

            def x1_stats(n, k, h):
                if k != 1 and h == 0:
                    dve.wait_ge(s["ln2_nmr"], 2 * (n - 1))
                dve.wait_ge(s["o_ev"], TP * (n - 1) + 2 * h + 2)
                stats(n - 1, st2, mv2, "ln2", h)

            def body(n, k):
                if runs(n, k, 0):
                    lo(cT[1][:], C_[:], cT[0][:], "c_hi", n + 1, "c_lo", XS)
                if runs(n, k, -1):
                    dve.wait_ge(s["ln1_nmr"], 2 * (n + 1))
                    if k == 0 or k == 1:
                        dve.wait_ge(s[("ld_x1", "ld_x2")[k]], 16)
                    for h in range(2):
                        stats(n + 1, st1, mv1, "ln1", h)
                if runs(n, k, 0):
                    for c in range(DC):
                        dve.wait_ge(s["q_hi"], DC * n + c + 1)
                        dve.scalar_tensor_tensor(qT[1][:, c, :], A_[:, c, :], bqk[:, c:c + 1], qT[0][:, c, :],
                                                 ALU.add, ALU.subtract).then_inc(s["q_lo"], 1)
                if runs(n, k, 1):
                    dve.wait_ge(s["s_exp"], TP * n)
                    dve.reciprocal(rinv[:], rsum[:]).then_inc(s["s_ri"], 1)
                    dve.wait_ge(s["s_ri"], n)
                    dve.tensor_scalar(rinvs[:], rinv[:], 1.0 / QS, None, ALU.mult).then_inc(s["s_ris"], 1)
                if runs(n, k, 0):
                    for c in range(DC):
                        dve.wait_ge(s["k_hi"], DC * n + c + 1)
                        dve.scalar_tensor_tensor(kT[1][:, c, :], D_[:, c, :], bqk[:, DC + c:DC + c + 1], kT[0][:, c, :],
                                                 ALU.add, ALU.subtract).then_inc(s["k_lo"], 1)
                if runs(n, k, 1):
                    for h in range(2):
                        lo(half(pT[1], h), by_half(B_, h), half(pT[0], h), "p_hi", 2 * (n - 1) + h + 1, "p_lo")
                if runs(n, k, 1):
                    dve.wait_ge(s["xbv"], n)
                    dve.wait_ge(s["s_ris"], n)
                    for t in range(TP):
                        if t % 2 == 0:
                            dve.wait_ge(s["o_mm"], TP * (n - 1) + t + 2)
                        xt = xres[:, bass.ds((n - 1) * TP + t, 1), :].rearrange("p o d -> p (o d)")
                        dve.scalar_tensor_tensor(xt, B_[:, t // 2, (t % 2) * D:(t % 2 + 1) * D], rinvs[:, t:t + 1], xt,
                                                 ALU.mult, ALU.add).then_inc(s["o_ev"], 1)
                        if k == NP and t % 2 == 1:
                            x1_stats(n, k, t // 2)
                if runs(n, k, 0):
                    lo(v[1][:], A_[:].rearrange("p a (b d) -> p (a b) d", d=D), v[0][:], "v_hi", n + 1, "v_lo")
                if runs(n, k, -1):
                    lo(xT[1][:], D_[:], xT[0][:], "x_hi", n + 2, "x_lo", XS)
                if runs(n, k, 2) and k not in (NP - 1, NP):
                    dve.wait_ge(s["l_mm"], 2 * (n - 1))
                    dve.tensor_copy(logit[:, tiles(n - 2), :].rearrange("p (h t) e -> p h (t e)", h=2),
                                    C_[:, :, 0:2 * E]).then_inc(s["l_ev"], 1)
                if runs(n, k, 1) and k != NP:
                    for h in range(2):
                        x1_stats(n, k, h)
                if runs(n, k, 2) and k == NP:
                    dve.wait_ge(s["l_mm"], 2 * (n - 1))
                    dve.tensor_copy(logit[:, tiles(n - 2), :].rearrange("p (h t) e -> p h (t e)", h=2),
                                    C_[:, :, 0:2 * E]).then_inc(s["l_ev"], 1)
                if k == NP:
                    for j in range(4):
                        w1_lo(0, j)
                    search_constants()
                if runs(n, k, 0):
                    for h in range(2):
                        tl = slice(2 * h, 2 * h + 2)
                        dve.wait_ge(s["s_mm"], 2 * n + h + 1)
                        dve.tensor_reduce(nmax[:, tl], B_[:, h, :].rearrange("p (b k) -> p b k", k=S), AX.X, ALU.max, negate=True).then_inc(s["s_max"], 1)
                        if k != 0 and h == 0:
                            dve.wait_ge(s["s_exp"], TP * n)
                        dve.wait_ge(s["s_max"], 2 * n + h + 1)
                        dve.tensor_scalar(nbias[:, tl], nmax[:, tl], SCORE, math.log(PS), ALU.mult, ALU.add).then_inc(s["s_nb"], 1)
                if runs(n, k, 2) and k == NP - 1:
                    dve.wait_ge(s["l_mm"], 2 * (n - 1))
                    dve.tensor_copy(logit[:, tiles(n - 2), :].rearrange("p (h t) e -> p h (t e)", h=2),
                                    C_[:, :, 0:2 * E]).then_inc(s["l_ev"], 1)

            phase_a(dve, body)

            dve.wait_ge(s["init_s"], 6)
            dve.wait_ge(s["key_ev"], 1)
            with dve.Fori(0, ROUNDS // UNROLL) as i:
                for j in range(UNROLL):
                    r = i * UNROLL + j
                    dve.wait_ge(s["srch_tr"], r + 1)
                    for c in range(3):
                        dve.tensor_scalar(junk[:, c], keyT[:], trial[:, c:c + 1].bitcast(F32), None, ALU.is_ge, ALU.add,
                                          accum_out=cnt[:, c:c + 1]).then_inc(s["srch_cmp"], 1)
                    dve.tensor_scalar(steps[:], steps[:], 2, None, ALU.logical_shift_right).then_inc(s["srch_step"], 1)
                    dve.wait_ge(s["srch_step"], r + 1)
                    dve.wait_ge(s["srch_mm"], r + 1)
                    dve.scalar_tensor_tensor(cand[:, 0:3], A_[:, 1, 0:3], float(K), trial[:].bitcast(F32), ALU.is_ge, ALU.mult).then_inc(s["srch_sel"], 1)
                    dve.wait_ge(s["srch_sel"], r + 1)
                    dve.tensor_reduce(cand[:, 3:4], cand[:], AX.X, ALU.max).then_inc(s["srch_base"], 1)
                    dve.wait_ge(s["srch_base"], r + 1)
                    dve.tensor_tensor(trial[:], steps[:], cand[:, 3:4].bitcast(I32).broadcast_to([P, 3]), ALU.bitwise_or).then_inc(s["srch_tr"], 1)
            dve.tensor_scalar(kth_q[:], pick[:], cand[:, 3:4], None, ALU.mult).then_inc(s["kq_s"], 1)
            for a, op in enumerate((ALU.is_gt, ALU.is_equal)):
                for h in range(2):
                    dve.tensor_scalar(junk[:, 2 * a + h, 0], keyT[:, h], cand[:, 3:4], None, op, ALU.add,
                                      accum_out=tot[:, a, h:h + 1]).then_inc(s["tot_s"], 1)
            dve.wait_ge(s["kq_mm"], 1)
            kb = A_[:, 0, 0:E].unsqueeze(1).broadcast_to([P, NT, E])
            dve.tensor_tensor(above[:, 0], gate[:], kb, ALU.is_gt).then_inc(s["above_s"], 1)
            dve.tensor_tensor(above[:, 1], gate[:], kb, ALU.is_equal).then_inc(s["above_s"], 1)
            dve.wait_ge(s["above_s"], 2)

            def split_places(c, e0, e1):
                dve.scalar_tensor_tensor(place[:, :, :, e0:e1].rearrange("p a t e -> p (a t) e"),
                                         B_[:, 0, :].rearrange("p (x e) -> p x e", e=E)[:, :, e0:e1], NOWHERE,
                                         above[:, :, :, e0:e1].rearrange("p a t e -> p (a t) e"),
                                         ALU.subtract, ALU.mult).then_inc(s["pos_a"], 1)
                dve.wait_ge(s["pos_a"], c)
                dve.scalar_tensor_tensor(pos[:, :, e0:e1], place[:, 0, :, e0:e1], NOWHERE, place[:, 1, :, e0:e1],
                                         ALU.add, ALU.add).then_inc(s["pos_s"], 1)
                dve.wait_ge(s["pos_s"], c)
                dve.tensor_scalar(loi[:, :, e0:e1], pos[:, :, e0:e1], P - 1, None, ALU.bitwise_and).then_inc(s["split_i"], 1)
                dve.tensor_scalar(hii[:, :, e0:e1], pos[:, :, e0:e1], int(math.log2(P)), None,
                                  ALU.logical_shift_right).then_inc(s["split_i"], 1)
                dve.wait_ge(s["split_i"], 2 * c)

            dve.wait_ge(s["pref_mm"], 1)
            split_places(1, 0, 1)

            def places(e, first):
                if not first:
                    dve.wait_ge(s["id_mm"], e)
                dve.tensor_copy(lo_e[:], loi[:, :, bass.ds(e, 1)].rearrange("p t o -> p (t o)")).then_inc(s["lo_s"], 1)
                dve.tensor_copy(hi_e[:], hii[:, :, bass.ds(e, 1)].rearrange("p t o -> p (t o)")).then_inc(s["hie_s"], 1)
                dve.wait_ge(s["hie_s"], e + 1)
                dve.tensor_tensor(inhi[:], iota8[:], hi_e[:, :].unsqueeze(2).broadcast_to([P, NT, KT]), ALU.is_equal).then_inc(s["hi_s"], 1)
                dve.wait_ge(s["hi_s"], e + 1)
                dve.tensor_tensor(val[:, :, 0, :], inhi[:], tileno[:], ALU.mult).then_inc(s["val_s"], 1)
                dve.tensor_scalar(val[:, :, 1, :], inhi[:], partno[:, 0:1], None, ALU.mult).then_inc(s["val_s"], 1)
                dve.wait_ge(s["lo_s"], e + 1)

            def onehot(k0, k1):
                dve.tensor_tensor(oneh[:, k0:k1, :], iota16[:, k0:k1, :], lo_e[:, :].unsqueeze(1).broadcast_to([P, k1 - k0, NT]),
                                  ALU.is_equal).then_inc(s["hot_s"], 1)

            def read_list(e, first, from_=D_):
                dve.wait_ge(s["id_mm"], e + 1)
                if not first:
                    dve.wait_ge(s["list_rdy"], e)
                dve.tensor_copy(idp[:], from_[:, 0, 0:2 * KT].rearrange("p (a t) -> p a t", a=2)).then_inc(s["id_ev"], 1)

            def ids_of(e, first):
                dve.wait_ge(s["id_ev"], e + 1)
                if not first:
                    dve.wait_ge(s["list_kept"], e)
                dve.scalar_tensor_tensor(ids[:], idp[:, 0, :], float(P), idp[:, 1, :], ALU.mult, ALU.add).then_inc(s["list_rdy"], 1)

            def keep(e, first):
                dve.wait_ge(s["gat_a"], 8 * KT * (e + 1))
                dve.wait_ge(s["gat_b"], 8 * KT * (e + 1))
                if not first:
                    dve.wait_ge(s["y_o"], KT * e)
                    dve.wait_ge(s["sc_done"], 16 * KT * e)
                dve.tensor_copy(ids_s[:], ids[:]).then_inc(s["list_kept"], 1)
                dve.tensor_copy(ge[:], ex[:, :, bass.ds(D + e, 1)].rearrange("p t o -> p (t o)")).then_inc(s["ge_s"], 1)
                dve.tensor_copy(b2e[:], b2_bc[:, bass.ds(e, 1), :].rearrange("p o d -> p (o d)")).then_inc(s["b2e_s"], 1)

            def b1_of(e, first):
                if not first:
                    dve.wait_ge(s["h_hi"], 2 * FC * e)
                dve.tensor_copy(b1e[:], bcol[:, bass.ds(e * FC, FC)]).then_inc(s["b1e_s"], 1)

            def w2_split(e, j, first):
                rows = slice(j * (FC // 4), (j + 1) * (FC // 4))
                if j == 0:
                    dve.wait_ge(s["ld_w2"], 16 * (e + 1))
                    if not first:
                        dve.wait_ge(s["y_mm"], KT * e)
                dve.tensor_scalar(w2[0][:, rows], w2r[:, rows], FS, None, ALU.mult).then_inc(s["w2_hi_s"], 1)
                dve.wait_ge(s["w2_hi_s"], 4 * e + j + 1)
                dve.scalar_tensor_tensor(w2[1][:, rows], w2r[:, rows], FS, w2[0][:, rows],
                                         ALU.mult, ALU.subtract).then_inc(s["w2_lo_s"], 1)

            def ex_lo(e, i):
                dve.wait_ge(s["ex_hi"], 4 * e + i + 1)
                span = slice((i // 2) * 512, (i // 2 + 1) * 512)
                dve.scalar_tensor_tensor(exT[1][:, i % 2, span], D_[:, i % 2, :], XS, exT[0][:, i % 2, span],
                                         ALU.mult, ALU.subtract).then_inc(s["ex_lo"], 1)

            def expert(e, first, next1, next2):
                b1_of(e, first)
                if not first and next1:
                    read_list(e + 1, False, D_)
                for u in range(2 * FC):
                    h, f = u // FC, u % FC
                    if first and u == SPLIT:
                        ex_lo(0, 2)
                        ex_lo(0, 3)
                        read_list(1, False, C_)
                    dve.wait_ge(s["h_hi"], 2 * FC * e + u + 1)
                    dve.tensor_tensor(hid[1][:, f, h * 512:(h + 1) * 512], g32[:, u % 2, :], hid[0][:, f, h * 512:(h + 1) * 512],
                                      ALU.subtract).then_inc(s["h_lo"], 1)
                    if u % 2 and u // 2 < 4:
                        w2_split(e, u // 2, first)
                    if u == KEEP:
                        keep(e, first)
                        if next1:
                            ids_of(e + 1, False)
                for t in range(KT):
                    dve.wait_ge(s["y_mm"], KT * e + t + 1)
                    if t == 0:
                        dve.wait_ge(s["b2e_s"], e + 1)
                    if not (first and t < 2):
                        dve.wait_ge(s["y_o"], KT * e + t - 1)
                    dve.scalar_tensor_tensor(yt[:, t % 2, :], C_[:, t % 2, 0:D], 1.0 / FS, b2e[:],
                                             ALU.mult, ALU.add).then_inc(s["y_t"], 1)
                    if next1 and t < 4:
                        w1_lo(e + 1, t)
                        ex_lo(e + 1, t)
                    if next2:
                        if t == 0:
                            places(e + 2, False)
                        elif t >= KT - 1 - HOTS:
                            if t < KT - 1:
                                j = t - (KT - 1 - HOTS)
                                onehot(P // HOTS * j, P // HOTS * (j + 1))

            def onehots():
                for j in range(HOTS):
                    onehot(P // HOTS * j, P // HOTS * (j + 1))

            places(0, True)
            dve.wait_ge(s["const3"], 1)
            onehots()
            read_list(0, True)
            ids_of(0, True)
            split_places(2, 1, E)
            places(1, False)
            onehots()
            dve.wait_ge(s["ld_b2"], 16 * E)
            for i in range(2):
                ex_lo(0, i)
            expert(0, True, True, True)
            with dve.Fori(1, E - 2) as e:
                expert(e, False, True, True)
            expert(E - 2, False, True, False)
            expert(E - 1, False, False, False)

        @block.tensor
        def _(pe):
            def pairs(out, lhs, rhs, chunks):
                terms = [(a, b, c) for c in range(chunks) for a, b in ((0, 0), (0, 1), (1, 0))]
                for i, (a, b, c) in enumerate(terms):
                    last = pe.matmul(out, lhs(a, c), rhs(b, c), start=i == 0, stop=i == len(terms) - 1)
                return last

            def transposes(out, src, t0, t1):
                for t in range(t0, t1):
                    for c in range(DC):
                        last = pe.transpose(out[:, c, t * P:(t + 1) * P], src[:, t, c * P:(c + 1) * P], ident[:])
                return last

            def x_transposes(n):
                for h in range(2):
                    pe.wait_ge(s["xn_rdy"], TP * n + 2 * h + 2)
                    last = transposes(D_, xn, 2 * h, 2 * h + 2)
                last.then_inc(s["x_tr"], 1)

            def half_T(out, src, h):
                for t in range(2):
                    for c in range(2):
                        last = pe.transpose(out[:, h, (2 * c + t) * P:(2 * c + t + 1) * P],
                                            src[:, 2 * h + t, c * P:(c + 1) * P], ident[:])
                return last

            wsp = [w_hi, w_lo]
            pe.wait_ge(s["const1"], 4)
            pe.wait_ge(s["ld_ctx"], 16)
            transposes(C_, ctx, 0, TP).then_inc(s["c_tr"], 1)
            pe.wait_ge(s["ld_b"], 48)
            NR = NB1 + 2 * DC
            pe.transpose(A_[:, 1, 0:NR], brow[:], ident[0:NR, 0:NR]).then_inc(s["b_tr"], 1)
            x_transposes(0)
            pe.wait_ge(s["w_lo_s"], 1)
            pe.wait_ge(s["b_col"], 1)

            def project_qk(n, k):
                pe.wait_ge(s["x_lo"], n + 1)
                if k != 0:
                    pe.wait_ge(s["v_lo"], n)
                for e in range(DC):
                    pairs(A_[:, e, :], lambda a, d: wsp[a][:, 0, d, e * P:(e + 1) * P],
                          lambda b, d: xT[b][:, d, :], DC).then_inc(s["q_mm"], 1)
                pe.wait_ge(s["c_lo"], n + 1)
                for e in range(DC):
                    pairs(D_[:, e, :], lambda a, d: wsp[a][:, 1, d, e * P:(e + 1) * P],
                          lambda b, d: cT[b][:, d, :], DC).then_inc(s["k_mm"], 1)

            def transpose_p(n, k):
                for h in range(2):
                    pe.wait_ge(s["s_exp"], TP * (n - 1) + 2 * h + 2)
                    half_T(B_, prob, h).then_inc(s["p_tr"], 1)

            def project_v(n, k):
                pe.wait_ge(s["q_lo"], DC * (n + 1))
                for t in range(TP):
                    last = pairs(A_[:, t // 2, (t % 2) * D:(t % 2 + 1) * D], lambda a, d: cT[a][:, d, t * P:(t + 1) * P],
                                 lambda b, d: wsp[b][:, 2, d, :], DC)
                last.then_inc(s["v_mm"], 1)

            def attend(n, k):
                pe.wait_ge(s["v_lo"], n)
                for t in range(TP):
                    if t % 2 == 0:
                        pe.wait_ge(s["p_lo"], 2 * (n - 1) + t // 2 + 1)
                    pairs(B_[:, t // 2, (t % 2) * D:(t % 2 + 1) * D], lambda a, c: pT[a][:, c, t * P:(t + 1) * P],
                          lambda b, c: v[b][:, (t // SC) * SC + c, :], SC).then_inc(s["o_mm"], 1)

            def transpose_x1(n, k):
                if k is not None and k >= NP:
                    pe.wait_ge(s["l_ev"], n - 2)
                for h in range(2):
                    pe.wait_ge(s["xn2_rdy"], TP * (n - 2) + 2 * h + 2)
                    half_T(C_, xn2, h).then_inc(s["x2_tr"], 1)

            def transpose_x(n, k):
                pe.wait_ge(s["k_lo"], DC * (n + 1))
                x_transposes(n + 1)

            def router(n, k):
                if k == 2:
                    pe.wait_ge(s["ld_wg"], 16)
                for t in range(TP):
                    if t % 2 == 0:
                        pe.wait_ge(s["x2_ev"], 2 * (n - 2) + t // 2 + 1)
                    for d in range(DC):
                        last = pe.matmul(C_[:, t // 2, (t % 2) * E:(t % 2 + 1) * E], xn2T[:, d, t * P:(t + 1) * P], wg[:, d, :],
                                         start=d == 0, stop=d == DC - 1)
                    if t % 2 == 1:
                        last.then_inc(s["l_mm"], 1)

            def score(n, k):
                pe.wait_ge(s["q_lo"], DC * (n + 1))
                pe.wait_ge(s["k_lo"], DC * (n + 1))
                for t in range(TP):
                    if k != 0 and t % 2 == 0:
                        pe.wait_ge(s["o_ev"], TP * (n - 1) + t + 2)
                    b0 = (t // SC) * S
                    last = pairs(B_[:, t // 2, (t % 2) * S:(t % 2 + 1) * S], lambda a, e: qT[a][:, e, t * P:(t + 1) * P],
                                 lambda b, e: kT[b][:, e, b0:b0 + S], DC)
                    if t % 2 == 1:
                        last.then_inc(s["s_mm"], 1)

            def transpose_ctx(n, k):
                pe.wait_ge(s["ld_ctx"], 16 * (n + 2))
                if k is None or k >= 2:
                    pe.wait_ge(s["l_ev"], n - 1)
                transposes(C_, ctx, 0, TP).then_inc(s["c_tr"], 1)

            def body(n, k):
                if runs(n, k, 0):
                    project_qk(n, k)
                if runs(n, k, 1):
                    transpose_p(n, k)
                if runs(n, k, 0):
                    project_v(n, k)
                if runs(n, k, 1):
                    attend(n, k)
                if runs(n, k, 2):
                    transpose_x1(n, k)
                if runs(n, k, -1):
                    transpose_x(n, k)
                if runs(n, k, 2) and k != NP - 1:
                    router(n, k)
                if runs(n, k, 0):
                    score(n, k)
                if k == NP - 1:
                    router(n, k)
                if runs(n, k, -1):
                    transpose_ctx(n, k)

            phase_a(pe, body)

            pe.wait_ge(s["l_ev"], NP)
            for h in range(2):
                last = pe.transpose(A_[:, 0, h * P:(h + 1) * P], logit[:, h * HT:(h + 1) * HT, :].rearrange("p t e -> p (t e)"), ident[:])
            last.then_inc(s["key_tr"], 1)
            pe.wait_ge(s["same_s"], 1)
            with pe.Fori(0, ROUNDS // UNROLL) as i:
                for j in range(UNROLL):
                    r = i * UNROLL + j
                    pe.wait_ge(s["srch_cmp"], 3 * (r + 1))
                    pe.matmul(A_[:, 1, 0:3], same16[:], cnt[:], start=True, stop=True).then_inc(s["srch_mm"], 1)
            pe.wait_ge(s["kq_s"], 1)
            pe.wait_ge(s["key_ev"], 1)
            pe.matmul(A_[:, 0, 0:E], onesf[:], kth_q[:], start=True, stop=True).then_inc(s["kq_mm"], 1)
            pe.wait_ge(s["tot_s"], 4)
            pe.wait_ge(s["early_s"], 2)
            order = order16[:].rearrange("q a p -> q (a p)")
            for j in range(4):
                pe.matmul(B_[:, 0, j * P:], tot[:, j // 2, j % 2:j % 2 + 1].broadcast_to([P, P]), order[:, 0:(4 - j) * P],
                          start=j == 0, stop=False)
            pe.wait_ge(s["above_s"], 2)
            pe.matmul(B_[:, 0, :], before16[:], above[:].rearrange("p a t e -> p (a t e)"), start=False, stop=True).then_inc(s["pref_mm"], 1)

            def list_of(e, first, to=D_):
                pe.wait_ge(s["val_s"], 2 * (e + 1))
                if not first:
                    pe.wait_ge(s["id_ev"], e)
                pe.wait_ge(s["hot_s"], HOTS * (e + 1))
                for t in range(NT):
                    last = pe.matmul(to[:, 0, 0:2 * KT], oneh[:, :, t], val[:, t].rearrange("p a j -> p (a j)"),
                                     start=t == 0, stop=t == NT - 1)
                last.then_inc(s["id_mm"], 1)

            def rows_T(e, i):
                pe.wait_ge(s["gat_a"] if i < 2 else s["gat_b"], 8 * KT * (e + 1))
                if i >= 2:
                    pe.wait_ge(s["ex_lo"], 4 * e + i - 1)
                for j in range(4):
                    last = pe.transpose(D_[:, i % 2, j * P:(j + 1) * P], ex[:, (i // 2) * 4 + j, (i % 2) * P:(i % 2 + 1) * P], ident[:])
                last.then_inc(s["ex_tr"], 1)

            def expert(e, first, next1, next2):
                pe.wait_ge(s["w1_lo_s"], 4 * (e + 1))
                for u in range(2 * FC):
                    h, f = u // FC, u % FC
                    if first and u == SPLIT:
                        rows_T(0, 2)
                        rows_T(0, 3)
                        list_of(1, False, C_)
                    if f == 0:
                        pe.wait_ge(s["ex_lo"], 4 * e + 2 * (h + 1))
                    if not (first and u < 4):
                        pe.wait_ge(s["h_hi"], 2 * FC * e + u - 3)
                    pairs(bank[(u % 4) // 2][:, u % 2, :], lambda a, c: w1[a][:, c, f * P:(f + 1) * P],
                          lambda b, c: exT[b][:, c, h * 512:(h + 1) * 512], DC).then_inc(s["h_mm"], 1)
                pe.wait_ge(s["w2_lo_s"], 4 * (e + 1))
                for t in range(KT):
                    if t % (KT // 2) == 0:
                        pe.wait_ge(s["h_lo"], 2 * FC * e + FC * (t // (KT // 2) + 1))
                    if not (first and t < 2):
                        pe.wait_ge(s["y_t"], KT * e + t - 1)
                    pairs(C_[:, t % 2, 0:D], lambda a, f: hid[a][:, f, t * P:(t + 1) * P],
                          lambda b, f: w2[b][:, f, :], FC).then_inc(s["y_mm"], 1)
                    if next1 and t < 4:
                        if t == 0:
                            pe.wait_ge(s["id_ev"], e + 2)
                        rows_T(e + 1, t)
                if next2:
                    pe.wait_ge(s["ex_lo"], 4 * (e + 2))
                    list_of(e + 2, False)

            pe.wait_ge(s["l_ev"], NP)
            list_of(0, True)
            pe.wait_ge(s["id_ev"], 1)
            for i in range(2):
                rows_T(0, i)
            expert(0, True, True, True)
            with pe.Fori(1, E - 2) as e:
                expert(e, False, True, True)
            expert(E - 2, False, True, False)
            expert(E - 1, False, False, False)


INS = ["x", "ctx_1024", "L0_xattn_Wq", "L0_xattn_bq", "L0_xattn_Wk", "L0_xattn_bk", "L0_xattn_Wv", "L0_xattn_bv",
       "L0_ffn_Wg", "L0_ffn_W1", "L0_ffn_b1", "L0_ffn_W2", "L0_ffn_b2"]


def kernel(**inputs):
    import concourse.bacc as bacc
    from concourse.bass_utils import run_bass_kernel_spmd

    nc = bacc.Bacc("TRN2", target_bir_lowering=False, num_devices=1)
    arrays, args = {}, []
    for name in INS:
        a = np.ascontiguousarray(inputs[name])
        arrays[f"in_{name}"] = a
        args.append(nc.dram_tensor(f"in_{name}", a.shape, mybir.dt.from_np(a.dtype), kind="ExternalInput").ap())
    out = nc.dram_tensor("out", inputs["x"].shape, F32, kind="ExternalOutput").ap()
    build(nc, *args, out)
    r = run_bass_kernel_spmd(nc, [arrays], core_ids=[0])
    return r.results[0]["out"]
```
